# Optimizing a Trainium2 kernel written in Bass

```python
import numpy as np
import jax
import jax.numpy as jnp

def _softmax(x, axis=-1):
    return jax.nn.softmax(x, axis=axis)

def _gelu(x):
    return jax.nn.gelu(x, approximate=True)

def _silu(x):
    return jax.nn.silu(x)

def _sigmoid(x):
    return jax.nn.sigmoid(x)

def _layernorm(x, axis=-1, eps=1e-05):
    m = jnp.mean(x, axis=axis, keepdims=True)
    v = jnp.var(x, axis=axis, keepdims=True)
    return (x - m) / jnp.sqrt(v + eps)

def _scatter_add(tgt, idx, src, axis=0):
    return tgt.at[idx].add(src)

def _segment_sum(src, seg, n):
    return jax.ops.segment_sum(src, seg, n)
kernel_name = 'mk_gnn_preln_d2_gnn_r8_b67702'

def setup_inputs(seed: int=0):
    np.random.seed(seed)
    _w = jnp.asarray

    def _rec_inputs():
        import jax
        import jax.numpy as jnp
        _gk = jax.random.key(seed)
        x = -0.0001006 + 1 * jax.random.normal(jax.random.fold_in(_gk, 1), (12500, 96), jnp.float32)
        src = jax.random.randint(jax.random.fold_in(_gk, 2), (200000,), 0, 12500, jnp.int32)
        dst = jax.random.randint(jax.random.fold_in(_gk, 3), (200000,), 0, 12500, jnp.int32)
        _o = jnp.argsort(dst, stable=True)
        src = src[_o]
        dst = dst[_o]
        edge_attr_32 = 0.000196303 + 1.00016 * jax.random.normal(jax.random.fold_in(_gk, 12), (200000, 32), jnp.float32)
        return (x, src, dst, edge_attr_32)
    x, src, dst, edge_attr_32 = _rec_inputs()

    def _L0_gnn_setup():
        import jax, jax.numpy as jnp
        import numpy as np
        N_NODES = 6250
        N_EDGES = 100000
        D_FEAT = 96
        L = 0.5
        key = jax.random.key(seed)
        k1, k2, k3 = jax.random.split(key, 3)
        h = jax.random.normal(k1, (N_NODES, D_FEAT), dtype=jnp.float32)
        src = jax.random.randint(k2, (N_EDGES,), 0, N_NODES, dtype=jnp.int64)
        dst = jax.random.randint(k3, (N_EDGES,), 0, N_NODES, dtype=jnp.int64)
        return {'h': h, 'src': src, 'dst': dst}
    _L0_gnn_all = _L0_gnn_setup()
    _L0_gnn_in = {k: v for k, v in _L0_gnn_all.items() if k in ()}
    del _L0_gnn_all

    def _L1_gnn_setup():
        import jax, jax.numpy as jnp
        import numpy as np
        N, E = (6250, 100000)
        DIN = DOUT = 96
        DE = 32

        def _egnn_conv(x, src, dst, edge_attr, W_msg, W_edge, W_root, b):
            msg = x[src] @ W_msg + edge_attr @ W_edge
            agg = jax.ops.segment_max(msg, dst, num_segments=x.shape[0])
            agg = jnp.where(jnp.isneginf(agg), 0.0, agg)
            return agg + x @ W_root + b
        key = jax.random.key(seed)
        ks = jax.random.split(key, 10)
        rn = lambda k, sh, sc: jax.random.normal(k, sh, jnp.float32) * sc
        return {'X': rn(ks[0], (N, DIN), 1.0), 'edge_index': jax.random.randint(ks[1], (2, E), 0, N, jnp.int32), 'edge_attr': rn(ks[2], (E, DE), 1.0), 'W1_msg': rn(ks[3], (DIN, DOUT), DIN ** (-0.5)), 'W1_edge': rn(ks[4], (DE, DOUT), DE ** (-0.5)), 'W1_root': rn(ks[5], (DIN, DOUT), DIN ** (-0.5)), 'b1': jnp.zeros((DOUT,), jnp.float32), 'W2_msg': rn(ks[6], (DOUT, DOUT), DOUT ** (-0.5)), 'W2_edge': rn(ks[7], (DE, DOUT), DE ** (-0.5)), 'W2_root': rn(ks[8], (DOUT, DOUT), DOUT ** (-0.5)), 'b2': jnp.zeros((DOUT,), jnp.float32)}
    _L1_gnn_all = _L1_gnn_setup()
    _L1_gnn_in = {k: v for k, v in _L1_gnn_all.items() if k in ('W1_msg', 'W1_edge', 'W1_root', 'b1', 'W2_msg', 'W2_edge', 'W2_root', 'b2')}
    del _L1_gnn_all
    return {'x': x, 'src': src, 'dst': dst, 'edge_attr_32': edge_attr_32, 'L1_gnn_W1_msg': _L1_gnn_in['W1_msg'], 'L1_gnn_W1_edge': _L1_gnn_in['W1_edge'], 'L1_gnn_W1_root': _L1_gnn_in['W1_root'], 'L1_gnn_b1': _L1_gnn_in['b1'], 'L1_gnn_W2_msg': _L1_gnn_in['W2_msg'], 'L1_gnn_W2_edge': _L1_gnn_in['W2_edge'], 'L1_gnn_W2_root': _L1_gnn_in['W2_root'], 'L1_gnn_b2': _L1_gnn_in['b2']}

def reference(x, src, dst, edge_attr_32, L1_gnn_W1_msg, L1_gnn_W1_edge, L1_gnn_W1_root, L1_gnn_b1, L1_gnn_W2_msg, L1_gnn_W2_edge, L1_gnn_W2_root, L1_gnn_b2):
    import jax
    import jax.numpy as jnp

    def _L0_gnn_ref(h, src, dst):
        import jax, jax.numpy as jnp
        import numpy as np
        N_NODES = 6250
        N_EDGES = 100000
        D_FEAT = 96
        L = 0.5
        N = h.shape[0]
        deg = jax.ops.segment_sum(jnp.ones_like(dst, dtype=h.dtype), dst, num_segments=N)
        inv_deg = (1.0 / jnp.maximum(deg, 1.0))[:, None]

        def mean_agg(x):
            msg_sum = jax.ops.segment_sum(x[src], dst, num_segments=N)
            return msg_sum * inv_deg
        neigh1 = mean_agg(h)
        neigh2 = mean_agg(neigh1)
        return L * neigh1 + (1.0 - L) * neigh2

    def _L1_gnn_ref(X, edge_index, edge_attr, W1_msg, W1_edge, W1_root, b1, W2_msg, W2_edge, W2_root, b2):
        import jax, jax.numpy as jnp
        import numpy as np
        N, E = (6250, 100000)
        DIN = DOUT = 96
        DE = 32

        def _egnn_conv(x, src, dst, edge_attr, W_msg, W_edge, W_root, b):
            msg = x[src] @ W_msg + edge_attr @ W_edge
            agg = jax.ops.segment_max(msg, dst, num_segments=x.shape[0])
            agg = jnp.where(jnp.isneginf(agg), 0.0, agg)
            return agg + x @ W_root + b
        src, dst = (edge_index[0], edge_index[1])
        c1 = jax.nn.leaky_relu(_egnn_conv(X, src, dst, edge_attr, W1_msg, W1_edge, W1_root, b1))
        c2 = jax.nn.leaky_relu(_egnn_conv(c1, src, dst, edge_attr, W2_msg, W2_edge, W2_root, b2))
        return c2
    edge_index = jnp.stack([src, dst])
    h = jnp.maximum(_layernorm(x, axis=-1), 0.0)
    x = x + _L0_gnn_ref(h, src, dst)
    h = jnp.maximum(_layernorm(x, axis=-1), 0.0)
    x = x + _L1_gnn_ref(h, edge_index, edge_attr_32, L1_gnn_W1_msg, L1_gnn_W1_edge, L1_gnn_W1_root, L1_gnn_b1, L1_gnn_W2_msg, L1_gnn_W2_edge, L1_gnn_W2_root, L1_gnn_b2)
    return x

_drawn_inputs = setup_inputs


def setup_inputs(seed=0):
    import zlib

    import numpy as np

    out = dict(_drawn_inputs(seed))
    spreads = {'L1_gnn_b1': (0.0, 0.308), 'L1_gnn_b2': (0.0, 0.31)}
    factors = {}
    for name, (base, spread) in spreads.items():
        noise = np.random.default_rng([zlib.crc32(name.encode()), seed]).standard_normal(out[name].shape)
        drawn = base * np.exp(spread * noise) if base else spread * noise
        out[name] = jnp.asarray(drawn.astype(out[name].dtype))
    for name, factor in factors.items():
        out[name] = (out[name] * factor).astype(out[name].dtype)
    return out
```

```python
from contextlib import ExitStack

import numpy as np

import concourse.bass as bass
from concourse import mybir

F32 = mybir.dt.float32
BF16 = mybir.dt.bfloat16
I32 = mybir.dt.int32
U32 = mybir.dt.uint32
ALU = mybir.AluOpType
ACT = mybir.ActivationFunctionType

P = 128
N, D = 12500, 96
E, DE = 200000, 32
COLS = E // P
REST = E - P * COLS
SHARE = COLS + 1
UNIT = 11
UNITS = COLS // UNIT
PAIRS = UNITS // 2
TILES = -(-N // P)
CHUNK = 7
CHUNKS = TILES // CHUNK
CPAIRS = CHUNKS // 2
FULL = N // TILES
LEFT = N - FULL * TILES
NPAD = P * TILES
BIG = float(np.finfo(np.float32).max)
EPS = 1e-5
SLOPE = 0.01
ROUNDS = 4
BANK = 512
MSG_COLS = (4, 4, 3)
TRICK = 12582912.0
PREP_META = 21
PREP_MAX = 39
DEG_ALL = 13
assert UNIT * UNITS == COLS and UNITS % 2 == 0 and CHUNK * CHUNKS == TILES and CHUNKS % 2 == 0
assert sum(MSG_COLS) == UNIT and REST == 64


def gnn(nc, x, src, dst, eat, eat_tail, wm1, we1, wr1, b1, wm2, we2, wr2, b2, out):
    with ExitStack() as ctx:
        def sb(name, shape, dt=F32):
            return ctx.enter_context(nc.sbuf_tensor(name, shape, dt))

        def sem(name):
            return ctx.enter_context(nc.semaphore(name))

        def sems(name, of, slots=0):
            one = (lambda n: [sem(f"{n}_slot{s}") for s in range(slots)]) if slots else sem
            return {k: one(f"{name}_{k}") for k in of}

        tables = [nc.dram_tensor(f"table{r}", (NPAD, D), F32).ap() for r in range(ROUNDS)]
        running = nc.dram_tensor("running", (E, D), F32).ap()

        src_sb = sb("src_sb", [P, SHARE], I32)
        dst_sb = sb("dst_sb", [P, SHARE], I32)
        dstf = sb("dstf", [P, SHARE])
        before_i = sb("before_i", [P, 1], I32)
        dst_hi = sb("dst_hi", [P, SHARE])
        scr = sb("scr", [P, SHARE])
        meta = sb("meta", [P, UNITS, 3, UNIT])
        meta_tail = sb("meta_tail", [P, 3])
        mflag = sb("mflag", [P, UNITS, UNIT])
        mflag_tail = sb("mflag_tail", [P, 1])
        idx_u = sb("idx_u", [P, 2, UNIT], U32)
        meta_u = sb("meta_u", [P, 2, 3, UNIT])
        rows_u = sb("rows_u", [P, 2, UNIT, D])
        run_u = sb("run_u", [P, 2, UNIT, D])
        hot_u = sb("hot_u", [P, 2, UNIT, P + TILES], BF16)
        eat_u = sb("eat_u", [DE, 2, UNIT, P])
        idx_t = sb("idx_t", [P, 1], U32)
        rows_t = sb("rows_t", [P, D])
        hot_t = sb("hot_t", [P, P + TILES], BF16)
        eat_t = sb("eat_t", [DE, REST])
        last = sb("last", [P, D])
        zero = sb("zero", [P, D])
        small = sb("small", [P, 16])
        pidx, pge, plen, pstart, same0, cnt, thru, mthru, msame0 = (small[:, k:k + 1] for k in range(9))
        before = small[:, 9:10]
        thrub = sb("thrub", [P, D])
        thrurow = sb("thrurow", [D, 2, P])
        carryT = sb("carryT", [D, P + 1])
        fix_idx = sb("fix_idx", [P, 1], U32)
        fix_in = sb("fix_in", [P, D])
        fix_out = sb("fix_out", [P, D])
        xs = sb("xs", [P, TILES * D])
        root = sb("root", [P, TILES * D])
        scale = sb("scale", [P, 3, TILES])
        deg = sb("deg", [P, TILES])
        ends = sb("ends", [P, TILES])
        onesT = sb("onesT", [P, TILES])
        end_idx = sb("end_idx", [P, TILES], U32)
        prefix = sb("prefix", [P, 1])
        nidx = sb("nidx", [P, 2, CHUNK], U32)
        nrows = sb("nrows", [P, 2, CHUNK, D])
        nout = sb("nout", [P, 2, CHUNK, D])
        hbuf = sb("hbuf", [P, 2, CHUNK, D])
        hT = sb("hT", [D + 1, 2, CHUNK * P])
        stats = sb("stats", [P, 2, CHUNK, 6])
        mv = sb("mv", [P, 2, CHUNK, 2])
        std = sb("std", [P, 2, CHUNK])
        rstd = sb("rstd", [P, 2, CHUNK])
        nbias = sb("nbias", [P, 2, CHUNK])
        eps = sb("eps", [P, 1])
        ident = sb("ident", [P, P])
        upper = sb("upper", [P, P])
        iota_b = sb("iota_b", [P, P], BF16)
        wcat = sb("wcat", [D + 1, 2, 2 * D])
        we = sb("we", [DE, 2, D])

        ps = ctx.enter_context(nc.psum_tensor("ps", [P, 8 * BANK], F32))
        HIST = 6 * BANK
        MISC = 7 * BANK
        CARRY = 5 * BANK
        OUTS = 2 * BANK

        rounds, convs, projected = range(ROUNDS), (2, 3), (1, 2)
        s_dst, s_src, s_w, s_tail = sem("dst_in"), sem("src_in"), sem("weights_in"), sem("tails_in")
        s_x = sems("x_in", range(CPAIRS))
        const, xpad = sem("constants_made"), sem("x_padding_made")
        pool_go, dve_go = sem("pool_goes_on"), sem("dve_goes_on")
        prep, dveinit = sem("prep_steps"), sem("dve_init")
        idx_ready, meta_ready = sems("idx_ready", rounds), sems("meta_ready", rounds)
        landed = sems("rows_landed", rounds, 2)
        eat_in = sems("edge_features_in", convs, 2)
        msg_ready, msg_added = sems("messages_ready", convs), sems("messages_added", convs)
        col_done = sems("column_reduced", rounds)
        stored = sems("running_stored", rounds, 2)
        tail_idx, tail_rows = sem("tail_idx_ready"), sems("tail_rows_landed", rounds)
        last_ready, last_stored = sems("last_ready", rounds), sems("last_stored", rounds)
        hot_ready, hot_used = sem("onehots_ready"), sem("onehots_used")
        deg_ready, deg_steps, total_ready = sem("degrees_ready"), sem("degree_steps"), sem("prefix_ready")
        thru_ready = sem("through_row_ready")
        lastT, scanned, carry = sems("lastT_ready", rounds), sems("carry_scanned", rounds), sems("carry_ready", rounds)
        fix_got, fix_made, fixed = sems("fix_row_landed", rounds), sems("fix_made", rounds), sems("row_fixed", rounds)
        nidx_ready, nlanded = sems("node_idx_ready", rounds), sems("node_rows_landed", rounds, 2)
        rows_added, scaled = sems("rows_added", rounds), sem("rows_scaled")
        stats_done, aggr_done, std_done = (sems(n, (0, 1)) for n in ("stats_done", "aggr_done", "std_done"))
        rstd_done, nbias_done, normed = (sems(n, (0, 1)) for n in ("rstd_done", "nbias_done", "normed"))
        act_done = sems("leaky_done", convs)
        ht_ps, ht_sb = sems("transposed", projected), sems("transposes_copied", projected)
        prod, out_sb = sems("products_ready", projected), sems("table_rows_ready", projected)
        root_sb = sems("root_ready", projected)
        out_ready = sem("output_ready")
        tstored = sems("table_stored", rounds, 2)
        out_stored = sem("output_stored")

        def shares(flat, width=1):
            a, b = flat[0:REST * SHARE * width], flat[REST * SHARE * width:E * width]
            return (a.rearrange("(p k) -> p k", p=REST), b.rearrange("(p k) -> p k", p=P - REST))

        run_flat = running.rearrange("e d -> (e d)")
        run_lo, run_hi = shares(run_flat, D)

        def table_view(t):
            return t.rearrange("(p t) d -> p (t d)", p=P)

        block = ctx.enter_context(nc.Block())

        @block.sync
        def _(sp):
            lo, hi = shares(dst)
            sp.dma_start(dst_sb[0:REST, :], lo).then_inc(s_dst, 16)
            sp.dma_start(dst_sb[REST:P, 0:COLS], hi).then_inc(s_dst, 16)
            lo = dst[SHARE - 1:SHARE - 1 + SHARE * (REST - 1)].rearrange("(p k) -> p k", k=SHARE)[:, 0:1]
            sp.wait_ge(dveinit, 1)
            sp.dma_start(before_i[1:REST, :], lo, allow_slow_non_contiguous=True).then_inc(s_dst, 16)
            base = REST * SHARE - 1
            hi = dst[base:base + COLS * (P - REST)].rearrange("(p k) -> p k", k=COLS)[:, 0:1]
            sp.dma_start(before_i[REST:P, :], hi, allow_slow_non_contiguous=True).then_inc(s_dst, 16)
            xv = x[0:FULL * TILES, :].rearrange("(p t) d -> p (t d)", t=TILES)
            sp.wait_ge(xpad, 1)
            W = 2 * CHUNK * D
            for g in range(CPAIRS):
                sp.dma_start(xs[0:112, g * W:(g + 1) * W], xv[0:112, g * W:(g + 1) * W]).then_inc(s_x[g], 16)
                sp.dma_start(xs[112:FULL, g * W:(g + 1) * W], xv[112:FULL, g * W:(g + 1) * W]).then_inc(s_x[g], 16)
                if g == 0:
                    xl = x[FULL * TILES:N, :].rearrange("(p t) d -> p (t d)", p=1)
                    sp.dma_start(xs[FULL:P, 0:LEFT * D], xl).then_inc(s_x[g], 16)

            for q in range(CHUNKS):
                sp.wait_ge(normed[0], q + 1)
                sp.dma_start(table_view(tables[0])[:, q * CHUNK * D:(q + 1) * CHUNK * D],
                             hbuf[:, q % 2].rearrange("p t d -> p (t d)")).then_inc(tstored[0][q % 2], 16)

            for r in range(ROUNDS):
                def pair(i):
                    for s in range(2):
                        sp.wait_ge(col_done[r], i * (2 * UNIT) + UNIT * (s + 1))
                        at = bass.ds((i * 2 + s) * (UNIT * D), UNIT * D)
                        sp.dma_start(run_lo[:, at], run_u[0:REST, s].rearrange("p k d -> p (k d)")
                                     ).then_inc(stored[r][s], 16)
                        sp.dma_start(run_hi[:, at], run_u[REST:P, s].rearrange("p k d -> p (k d)")
                                     ).then_inc(stored[r][s], 16)

                with sp.Fori(0, PAIRS) as i:
                    pair(i)
                sp.wait_ge(last_ready[r], 2)
                sp.dma_start(run_lo[:, COLS * D:SHARE * D], last[0:REST, :]).then_inc(last_stored[r], 16)

                if r < ROUNDS - 1:
                    done = scaled if r == 0 else out_sb[r]
                    with sp.Fori(0, CPAIRS) as i:
                        for s in range(2):
                            sp.wait_ge(done, i * 2 + (s + 1))
                            sp.dma_start(table_view(tables[r + 1])[:, bass.ds((i * 2 + s) * (CHUNK * D), CHUNK * D)],
                                         nout[:, s].rearrange("p t d -> p (t d)")).then_inc(tstored[r + 1][s], 16)
                else:
                    ov = out[0:FULL * TILES, :].rearrange("(p t) d -> p (t d)", t=TILES)
                    with sp.Fori(0, CHUNKS) as q:
                        sp.wait_ge(out_ready, q + 1)
                        at = bass.ds(q * (CHUNK * D), CHUNK * D)
                        sp.dma_start(ov[0:112, at], xs[0:112, at]).then_inc(out_stored, 16)
                        sp.dma_start(ov[112:FULL, at], xs[112:FULL, at]).then_inc(out_stored, 16)
                    sp.dma_start(out[FULL * TILES:N, :].rearrange("(p t) d -> p (t d)", p=1),
                                 xs[FULL:P, 0:LEFT * D]).then_inc(out_stored, 16)
                    sp.wait_ge(out_stored, 16 * (2 * CHUNKS + 1))

        @block.gpsimd
        def _(pool):
            pool.memset(ident[:], 0.0).then_inc(const, 1)
            pool.memset(upper[:], 1.0).then_inc(const, 1)
            pool.wait_ge(const, 2)
            pool.affine_select(out=ident[:], in_=ident[:], compare_op=ALU.not_equal, fill=1.0, base=0,
                               pattern=[[-1, P]], channel_multiplier=1).then_inc(const, 1)
            pool.affine_select(out=upper[:], in_=upper[:], compare_op=ALU.is_gt, fill=0.0, base=0,
                               pattern=[[1, P]], channel_multiplier=-1).then_inc(const, 1)
            pool.iota(iota_b[:], pattern=[[1, P]], base=0, channel_multiplier=0,
                      allow_small_or_imprecise_dtypes=True).then_inc(const, 1)
            pool.iota(pidx, pattern=[[0, 1]], base=0, channel_multiplier=1,
                      allow_small_or_imprecise_dtypes=True).then_inc(const, 1)

            def gather(to, table, idx):
                return pool.indirect_dma_start(to, None, table[:, :], bass.IndirectOffsetOnAxis(idx, 0))

            for r in range(ROUNDS):
                for s in range(2):
                    pool.wait_ge(tstored[r][s], 16 * CPAIRS)

                def pair(i, first):
                    for s in range(2):
                        pool.wait_ge(idx_ready[r], i * 2 + (s + 1))
                        if not first:
                            pool.wait_ge(col_done[r], i * (2 * UNIT) + UNIT * (s + 1) - 2 * UNIT)
                        pool.sem_inc(pool_go, 1)
                        for c in range(UNIT):
                            gather(rows_u[:, s, c, :], tables[r], idx_u[:, s, c:c + 1]).then_inc(landed[r][s], 16)

                pair(0, True)
                with pool.Fori(1, PAIRS) as i:
                    pair(i, False)
                if r == 0:
                    pool.wait_ge(tail_idx, 1)
                else:
                    pool.wait_ge(last_ready[r - 1], 2)
                gather(rows_t[0:REST, :], tables[r], idx_t[0:REST, :]).then_inc(tail_rows[r], 16)

                for s in range(2):
                    pool.wait_ge(stored[r][s], 32 * PAIRS)
                pool.wait_ge(last_stored[r], 16)
                gather(fix_in[:, :], running, fix_idx[:, :]).then_inc(fix_got[r], 16)
                pool.wait_ge(fix_made[r], 1)
                pool.indirect_dma_start(running[:, :], bass.IndirectOffsetOnAxis(fix_idx[:, :], 0),
                                        fix_out[:, :], None).then_inc(fixed[r], 16)
                pool.wait_ge(fixed[r], 16)

                def npair(i, first):
                    for s in range(2):
                        pool.wait_ge(nidx_ready[r], i * 2 + (s + 1))
                        if not first:
                            if r < 2:
                                pool.wait_ge(rows_added[r], i * (2 * CHUNK) + CHUNK * (s + 1) - 2 * CHUNK)
                            else:
                                pool.wait_ge(act_done[r], i * 2 + (s + 1) - 2)
                            if r == 0:
                                pool.wait_ge(scaled, i * 2 + (s + 1) - 2)
                        pool.sem_inc(pool_go, 1)
                        for j in range(CHUNK):
                            gather(nrows[:, s, j, :], running, nidx[:, s, j:j + 1]).then_inc(nlanded[r][s], 16)

                npair(0, True)
                with pool.Fori(1, CPAIRS) as i:
                    npair(i, False)

        @block.scalar
        def _(act):
            lo, hi = shares(src)
            act.dma_start(src_sb[0:REST, :], lo).then_inc(s_src, 16)
            act.dma_start(src_sb[REST:P, 0:COLS], hi).then_inc(s_src, 16)
            act.wait_ge(dveinit, 2)
            for k, (wm, wr, b, wed) in enumerate(((wm1, wr1, b1, we1), (wm2, wr2, b2, we2))):
                act.dma_start(wcat[0:D, k, 0:D], wm).then_inc(s_w, 16)
                act.dma_start(wcat[0:D, k, D:2 * D], wr).then_inc(s_w, 16)
                act.dma_start(wcat[D:D + 1, k, D:2 * D], b.rearrange("(a d) -> a d", a=1)).then_inc(s_w, 16)
                act.dma_start(we[:, k, :], wed).then_inc(s_w, 16)
            act.dma_start(eat_t[:, :], eat_tail).then_inc(s_tail, 16)
            act.wait_ge(s_src, 32)
            act.copy(idx_t[0:REST, :], src_sb[0:REST, COLS:SHARE]).then_inc(tail_idx, 1)

            def norm(k, q, s, first):
                act.wait_ge(aggr_done[k], q * CHUNK + CHUNK)
                if not first:
                    act.wait_ge(rstd_done[k], q - 1)
                act.activation(std[:, s], mv[:, s, :, 1], ACT.Sqrt, bias=eps[:, 0:1]).then_inc(std_done[k], 1)
                act.wait_ge(nbias_done[k], q + 1)
                if not first:
                    if k == 0:
                        act.wait_ge(tstored[0][s], (q // 2) * 16)
                    else:
                        act.wait_ge(ht_ps[1], q - 1)
                for j in range(CHUNK):
                    if k == 0:
                        at = xs[:, q * CHUNK * D + j * D:q * CHUNK * D + (j + 1) * D]
                    else:
                        at = xs[:, bass.ds(q * (CHUNK * D) + j * D, D)]
                    i = act.activation(hbuf[:, s, j, :], at, ACT.Relu, bias=nbias[:, s, j:j + 1],
                                       scale=rstd[:, s, j:j + 1])
                i.then_inc(normed[k], 1)

            for q in range(CHUNKS):
                norm(0, q, q % 2, q < 2)

            for r in range(ROUNDS):
                def stage(i, first):
                    for s in range(2):
                        if not first:
                            act.wait_ge(landed[r][s], i * (16 * UNIT))
                        act.copy(idx_u[:, s, :], src_sb[:, bass.ds((i * 2 + s) * UNIT, UNIT)]).then_inc(idx_ready[r], 1)
                        if not first:
                            act.wait_ge(col_done[r], i * (2 * UNIT) + UNIT * (s + 1) - 2 * UNIT)
                        if r == 0:
                            if first and s == 0:
                                act.wait_ge(prep, PREP_META)
                            act.copy(meta_u[:, s].rearrange("p a k -> p (a k)"),
                                     meta.rearrange("p u a k -> p (u a k)")[:, bass.ds((i * 2 + s) * (3 * UNIT), 3 * UNIT)]
                                     ).then_inc(meta_ready[r], 1)
                        else:
                            if r == 2 and first and s == 0:
                                act.wait_ge(prep, PREP_MAX)
                            flags = meta[:, bass.ds(i * 2 + s, 1), 0, :] if r == 1 else mflag[:, bass.ds(i * 2 + s, 1), :]
                            act.copy(meta_u[:, s, 0:1, :], flags).then_inc(meta_ready[r], 1)
                        if r >= 2:
                            if not first:
                                act.wait_ge(msg_ready[r], i * 2 + (s + 1) - 2)
                            act.dma_start(eat_u[:, s].rearrange("f k p -> f (k p)"),
                                          eat[:, bass.ds((i * 2 + s) * (UNIT * P), UNIT * P)]).then_inc(eat_in[r][s], 16)

                stage(0, True)
                with act.Fori(1, PAIRS) as i:
                    stage(i, False)

                def nstage(q, s):
                    act.copy(nidx[:, s, :], end_idx[:, bass.ds(q * CHUNK, CHUNK)]).then_inc(nidx_ready[r], 1)

                def node(i, first, more):
                    for s in range(2):
                        q = i * 2 + s
                        act.wait_ge(nlanded[r][s], i * (16 * CHUNK) + 16 * CHUNK)
                        if more:
                            nstage(q + 2, s)
                        if r == 0:
                            if not first:
                                act.wait_ge(tstored[1][s], i * 16)
                            for j in range(CHUNK):
                                m = act.activation(nout[:, s, j, :], nrows[:, s, j, :], ACT.Copy,
                                                   scale=scale[:, 0, bass.ds(q * CHUNK + j, 1)])
                            m.then_inc(scaled, 1)
                        if r == 1:
                            norm(1, q, s, first)
                        if r in (1, 2):
                            act.wait_ge(ht_ps[r], q + 1)
                            act.copy(hT[0:D, s, :], ps[0:D, 0:CHUNK * P]).then_inc(ht_sb[r], 1)
                            act.wait_ge(prod[r], q + 1)
                            if not first:
                                act.wait_ge(tstored[r + 1][s], i * 16)
                            pv = ps[:, OUTS:OUTS + CHUNK * 256].rearrange("p (t c) -> p t c", t=CHUNK)
                            act.copy(nout[:, s], pv[:, :, 0:D]).then_inc(out_sb[r], 1)
                            if r == 2:
                                act.wait_ge(rows_added[2], q * CHUNK + CHUNK)
                            act.copy(root[:, bass.ds(q * (CHUNK * D), CHUNK * D)].rearrange("p (t d) -> p t d", t=CHUNK),
                                     pv[:, :, D:2 * D]).then_inc(root_sb[r], 1)

                if r == 0:
                    act.wait_ge(deg_steps, DEG_ALL)
                nstage(0, 0)
                nstage(1, 1)
                node(0, True, True)
                with act.Fori(1, CPAIRS - 1) as i:
                    node(i, False, True)
                node(CPAIRS - 1, False, False)

        @block.tensor
        def _(pe):
            pe.wait_ge(const, 6)

            def hist(i, first):
                for s in range(2):
                    pe.wait_ge(hot_ready, i * (4 * UNIT) + 2 * UNIT * (s + 1))
                    for c in range(UNIT):
                        m = pe.matmul(ps[:, HIST:HIST + TILES], hot_u[:, s, c, 0:P], hot_u[:, s, c, P:P + TILES],
                                      start=(first and s == 0 and c == 0), stop=False, skip_group_check=True)
                    m.then_inc(hot_used, 1)

            hist(0, True)
            with pe.Fori(1, PAIRS) as i:
                hist(i, False)
            pe.wait_ge(hot_ready, 4 * UNIT * PAIRS + 2)
            pe.matmul(ps[:, HIST:HIST + TILES], hot_t[0:REST, 0:P], hot_t[0:REST, P:P + TILES],
                      start=False, stop=True, skip_group_check=True).then_inc(deg_ready, 1)
            pe.wait_ge(deg_steps, 2)
            pe.matmul(ps[:, MISC + 256:MISC + 257], upper[:, :], ends[:, TILES - 1:TILES],
                      start=True, stop=True).then_inc(total_ready, 1)
            pe.wait_ge(prep, PREP_MAX)
            pe.matmul(ps[0:D, MISC + 384:MISC + 384 + P], thrub[:, :], ident[:, :],
                      start=True, stop=True).then_inc(thru_ready, 1)

            for r in range(ROUNDS):
                if r >= 2:
                    k = r - 2
                    if r == 2:
                        pe.wait_ge(s_tail, 16)

                    def messages(i, first):
                        for s in range(2):
                            pe.wait_ge(eat_in[r][s], i * 16 + 16)
                            if not first:
                                pe.wait_ge(msg_added[r], i * (2 * 3) + 3 * (s + 1) - 6)
                            c = 0
                            for b, n in enumerate(MSG_COLS):
                                for j in range(n):
                                    at = (3 * s + b) * BANK + j * D
                                    m = pe.matmul(ps[:, at:at + D], eat_u[:, s, c, :], we[:, k, :],
                                                  start=True, stop=True)
                                    c += 1
                            m.then_inc(msg_ready[r], 1)

                    pe.wait_ge(root_sb[r - 1] if r == 2 else root_sb[2], CHUNKS)
                    messages(0, True)
                    with pe.Fori(1, PAIRS) as i:
                        messages(i, False)
                    pe.wait_ge(msg_added[r], 3 * UNITS)
                    pe.matmul(ps[0:REST, 0:D], eat_t[:, :], we[:, k, :], start=True, stop=True).then_inc(msg_ready[r], 1)

                pe.wait_ge(last_ready[r], 2)
                pe.transpose(ps[0:D, CARRY:CARRY + P], last[:, :], ident[:, :]).then_inc(lastT[r], 1)
                pe.wait_ge(scanned[r], 1)
                pe.transpose(ps[:, CARRY + P:CARRY + P + D], carryT[:, 0:P], ident[0:D, 0:D]).then_inc(carry[r], 1)

                if r in (1, 2):
                    k = r - 1
                    ready = normed[1] if r == 1 else act_done[2]
                    if r == 1:
                        pe.wait_ge(s_w, 16 * 8)

                    def products(i, first):
                        for s in range(2):
                            q = i * 2 + s
                            pe.wait_ge(ready, q + 1)
                            if not (first and s == 0):
                                pe.wait_ge(ht_sb[r], q)
                            for j in range(CHUNK):
                                m = pe.transpose(ps[0:D, j * P:(j + 1) * P], hbuf[:, s, j, :], ident[:, :])
                            m.then_inc(ht_ps[r], 1)
                            pe.wait_ge(ht_sb[r], q + 1)
                            if not (first and s == 0):
                                pe.wait_ge(root_sb[r], q)
                            for j in range(CHUNK):
                                m = pe.matmul(ps[:, OUTS + 256 * j:OUTS + 256 * j + 2 * D],
                                              hT[:, s, j * P:(j + 1) * P], wcat[:, k, :], start=True, stop=True)
                            m.then_inc(prod[r], 1)

                    products(0, True)
                    with pe.Fori(1, CPAIRS) as i:
                        products(i, False)

        @block.vector
        def _(dve):
            steps = [0]

            def step(ins):
                steps[0] += 1
                ins.then_inc(prep, 1)
                dve.wait_ge(prep, steps[0])

            dve.memset(before_i[:], -1).then_inc(dveinit, 1)
            dve.memset(wcat[:], 0.0).then_inc(dveinit, 1)
            dve.memset(xs[FULL // 32 * 32:P, LEFT * D:], 0.0).then_inc(xpad, 1)
            step(dve.memset(eps[:], EPS))
            step(dve.memset(hT[D:D + 1], 1.0))
            step(dve.memset(zero[:], 0.0))
            step(dve.memset(onesT[:], 1.0))
            step(dve.memset(carryT[:, 0:1], 0.0))
            step(dve.memset(dstf[:], -1.0))
            dve.wait_ge(s_dst, 64)
            dve.wait_ge(const, 6)
            step(dve.tensor_copy(dstf[:, 0:COLS], dst_sb[:, 0:COLS]))
            step(dve.tensor_copy(dstf[0:REST, COLS:], dst_sb[0:REST, COLS:]))
            step(dve.tensor_copy(before, before_i[:]))
            flat = meta[:, :, 0, :]
            step(dve.tensor_tensor(scr[:, 1:], dstf[:, 1:], dstf[:, 0:COLS], ALU.is_equal))
            step(dve.memset(scr[:, 0:1], 0.0))
            step(dve.tensor_copy(flat, scr[:, 0:COLS].rearrange("p (u k) -> p u k", k=UNIT)))
            step(dve.tensor_copy(meta_tail[:, 0:1], scr[:, COLS:]))
            step(dve.tensor_scalar(scr[:], dstf[:], -(TILES - 1) / 2, 1.0 / TILES, ALU.add, ALU.mult))
            step(dve.tensor_scalar(scr[:], scr[:], TRICK, None, ALU.add))
            step(dve.tensor_scalar(dst_hi[:], scr[:], -TRICK, None, ALU.add))
            step(dve.scalar_tensor_tensor(scr[:], dst_hi[:], -float(TILES), dstf[:], ALU.mult, ALU.add))
            step(dve.tensor_copy(meta[:, :, 1, :], scr[:, 0:COLS].rearrange("p (u k) -> p u k", k=UNIT)))
            step(dve.tensor_copy(meta_tail[:, 1:2], scr[:, COLS:]))
            step(dve.tensor_copy(meta[:, :, 2, :], dst_hi[:, 0:COLS].rearrange("p (u k) -> p u k", k=UNIT)))
            step(dve.tensor_copy(meta_tail[:, 2:3], dst_hi[:, COLS:]))
            assert steps[0] == PREP_META

            def stats_of(k, q, s, first):
                if not first:
                    dve.wait_ge(nbias_done[k], q - 1)
                    dve.wait_ge(std_done[k], q - 1)
                dve.sem_inc(dve_go, 1)
                for j in range(CHUNK):
                    if k == 0:
                        at = xs[:, q * CHUNK * D + j * D:q * CHUNK * D + (j + 1) * D]
                    else:
                        at = xs[:, bass.ds(q * (CHUNK * D) + j * D, D)]
                    dve.bn_stats(stats[:, s, j, :], at).then_inc(stats_done[k], 1)
                for j in range(CHUNK):
                    dve.wait_ge(stats_done[k], q * CHUNK + j + 1)
                    dve.sem_inc(dve_go, 1)
                    dve.bn_aggr(mv[:, s, j, :], stats[:, s, j, :]).then_inc(aggr_done[k], 1)

            def invert(k, q, s, first):
                dve.wait_ge(std_done[k], q + 1)
                if not first:
                    dve.wait_ge(normed[k], q - 1)
                dve.reciprocal(rstd[:, s], std[:, s]).then_inc(rstd_done[k], 1)
                dve.wait_ge(rstd_done[k], q + 1)
                dve.scalar_tensor_tensor(nbias[:, s], mv[:, s, :, 0], -1.0, rstd[:, s], ALU.mult,
                                         ALU.mult).then_inc(nbias_done[k], 1)

            for q in range(CHUNKS):
                if q % 2 == 0:
                    dve.wait_ge(s_x[q // 2], 48 if q == 0 else 32)
                stats_of(0, q, q % 2, q < 2)
                invert(0, q, q % 2, q < 2)

            step(dve.tensor_tensor(same0, dstf[:, 0:1], before, ALU.is_equal))
            step(dve.tensor_scalar(scr[:], dstf[:], dstf[:, 0:1], None, ALU.is_equal))
            step(dve.reduce_sum(cnt, scr[:], mybir.AxisListType.X))
            step(dve.tensor_scalar(pge, pidx, float(REST), None, ALU.is_ge))
            step(dve.tensor_scalar(plen, pge, -1.0, float(SHARE), ALU.mult, ALU.add))
            step(dve.tensor_scalar(pstart, pidx, float(REST), None, ALU.min))
            step(dve.scalar_tensor_tensor(pstart, pidx, float(COLS), pstart, ALU.mult, ALU.add))
            step(dve.scalar_tensor_tensor(pstart, cnt, -1.0, pstart, ALU.add, ALU.add))
            step(dve.tensor_copy(fix_idx[:], pstart))
            step(dve.tensor_tensor(thru, cnt, plen, ALU.is_equal))
            step(dve.tensor_tensor(thru, thru, same0, ALU.mult))
            step(dve.tensor_scalar(thrub[:], zero[:], thru, None, ALU.add))
            for a, b in ((mflag, meta[:, :, 0, :]), (mflag_tail, meta_tail[:, 0:1]), (msame0, same0)):
                a = a if a is msame0 else a[:]
                step(dve.tensor_scalar(a, b, 2.0, -1.0, ALU.mult, ALU.add))
                step(dve.tensor_scalar(a, a, BIG, None, ALU.mult))
            assert steps[0] == PREP_MAX

            for r in range(ROUNDS):
                op0, op1 = (ALU.mult, ALU.add) if r < 2 else (ALU.min, ALU.max)

                def pair(i, first):
                    for s in range(2):
                        dve.wait_ge(meta_ready[r], i * 2 + (s + 1))
                        if r == 0:
                            if not first:
                                dve.wait_ge(hot_used, i * 2 + (s + 1) - 2)
                            for c in range(UNIT):
                                dve.tensor_scalar(hot_u[:, s, c, 0:P], iota_b[:, :], meta_u[:, s, 2, c:c + 1],
                                                  None, ALU.is_equal).then_inc(hot_ready, 1)
                                dve.tensor_scalar(hot_u[:, s, c, P:P + TILES], iota_b[:, 0:TILES],
                                                  meta_u[:, s, 1, c:c + 1], None, ALU.is_equal).then_inc(hot_ready, 1)
                        dve.wait_ge(landed[r][s], i * (16 * UNIT) + 16 * UNIT)
                        if r >= 2:
                            dve.wait_ge(msg_ready[r], i * 2 + (s + 1))
                            c = 0
                            for b, n in enumerate(MSG_COLS):
                                at = (3 * s + b) * BANK
                                rows = rows_u[:, s, c:c + n, :].rearrange("p k d -> p (k d)")
                                dve.tensor_tensor(rows, rows, ps[:, at:at + n * D], ALU.add).then_inc(msg_added[r], 1)
                                c += n
                            dve.wait_ge(msg_added[r], i * 6 + 3 * (s + 1))
                        if not first:
                            dve.wait_ge(stored[r][s], i * 32)
                        for c in range(UNIT):
                            if first and s == 0 and c == 0:
                                prev = zero[:, :]
                            else:
                                prev = run_u[:, s, c - 1, :] if c else run_u[:, 1 - s, UNIT - 1, :]
                                dve.wait_ge(col_done[r], i * (2 * UNIT) + (UNIT * s + c))
                            dve.scalar_tensor_tensor(run_u[:, s, c, :], prev, meta_u[:, s, 0, c:c + 1],
                                                     rows_u[:, s, c, :], op0, op1).then_inc(col_done[r], 1)

                pair(0, True)
                with dve.Fori(1, PAIRS) as i:
                    pair(i, False)

                if r == 0:
                    dve.tensor_scalar(hot_t[:, 0:P], iota_b[:, :], meta_tail[:, 2:3], None,
                                      ALU.is_equal).then_inc(hot_ready, 1)
                    dve.tensor_scalar(hot_t[:, P:P + TILES], iota_b[:, 0:TILES], meta_tail[:, 1:2], None,
                                      ALU.is_equal).then_inc(hot_ready, 1)
                dve.wait_ge(col_done[r], COLS)
                if r >= 1:
                    dve.wait_ge(lastT[r - 1], 1)
                    dve.wait_ge(last_stored[r - 1], 16)
                dve.tensor_copy(last[REST:P, :], run_u[REST:P, 1, UNIT - 1, :]).then_inc(last_ready[r], 1)
                dve.wait_ge(tail_rows[r], 16)
                if r >= 2:
                    dve.wait_ge(msg_ready[r], UNITS + 1)
                    dve.tensor_tensor(rows_t[0:REST, :], rows_t[0:REST, :], ps[0:REST, 0:D],
                                      ALU.add).then_inc(msg_added[r], 1)
                    dve.wait_ge(msg_added[r], 3 * UNITS + 1)
                flag = meta_tail[0:REST, 0:1] if r < 2 else mflag_tail[0:REST, :]
                dve.scalar_tensor_tensor(last[0:REST, :], run_u[0:REST, 1, UNIT - 1, :], flag, rows_t[0:REST, :],
                                         op0, op1).then_inc(last_ready[r], 1)

                if r == 0:
                    dve.wait_ge(deg_ready, 1)
                    dve.tensor_copy(deg[:], ps[:, HIST:HIST + TILES]).then_inc(deg_steps, 1)
                    dve.wait_ge(deg_steps, 1)
                    dve.tensor_tensor_scan(ends[:], onesT[:], deg[:], 0.0, ALU.mult, ALU.add).then_inc(deg_steps, 1)
                    dve.tensor_scalar(scale[:, 0, :], deg[:], 1.0, None, ALU.max).then_inc(deg_steps, 1)
                    dve.tensor_scalar(scale[:, 2, :], deg[:], 1.0, None, ALU.min).then_inc(deg_steps, 1)
                    dve.wait_ge(deg_steps, 4)
                    dve.reciprocal(scale[:, 1, :], scale[:, 0, :]).then_inc(deg_steps, 1)
                    dve.wait_ge(total_ready, 1)
                    dve.wait_ge(thru_ready, 1)
                    dve.tensor_copy(prefix[:], ps[:, MISC + 256:MISC + 257]).then_inc(deg_steps, 1)
                    dve.wait_ge(deg_steps, 6)
                    dve.tensor_tensor(scale[:, 0, :], scale[:, 1, :], scale[:, 2, :], ALU.mult).then_inc(deg_steps, 1)
                    dve.tensor_scalar(ends[:], ends[:], prefix[:, 0:1], -1.0, ALU.add, ALU.add).then_inc(deg_steps, 1)
                    dve.wait_ge(deg_steps, 8)
                    dve.tensor_scalar(scale[:, 1, :], scale[:, 0, :], 0.5, None, ALU.mult).then_inc(deg_steps, 1)
                    dve.tensor_scalar(end_idx[:], ends[:], 0.0, None, ALU.max).then_inc(deg_steps, 1)
                    dve.tensor_copy(thrurow[:, 0, :], ps[0:D, MISC + 384:MISC + 384 + P]).then_inc(deg_steps, 1)
                    dve.wait_ge(deg_steps, 11)
                    dve.tensor_scalar(thrurow[:, 1, :], thrurow[:, 0, :], 2.0, -1.0, ALU.mult, ALU.add).then_inc(deg_steps, 1)
                    dve.wait_ge(deg_steps, 12)
                    dve.tensor_scalar(thrurow[:, 1, :], thrurow[:, 1, :], BIG, None, ALU.mult).then_inc(deg_steps, 1)
                    dve.wait_ge(deg_steps, DEG_ALL)

                dve.wait_ge(lastT[r], 1)
                if r >= 1:
                    dve.wait_ge(carry[r - 1], 1)
                dve.tensor_tensor_scan(carryT[:, 1:P + 1], thrurow[:, r // 2, :], ps[0:D, CARRY:CARRY + P], 0.0,
                                       op0, op1).then_inc(scanned[r], 1)
                dve.wait_ge(carry[r], 1)
                dve.wait_ge(fix_got[r], 16)
                dve.scalar_tensor_tensor(fix_out[:], ps[:, CARRY + P:CARRY + P + D], same0 if r < 2 else msame0,
                                         fix_in[:], op0, op1).then_inc(fix_made[r], 1)

                def node(i, first):
                    for s in range(2):
                        q = i * 2 + s
                        here = bass.ds(q * (CHUNK * D), CHUNK * D)
                        dve.wait_ge(nlanded[r][s], i * (16 * CHUNK) + 16 * CHUNK)
                        if r < 2:
                            for j in range(CHUNK):
                                at = xs[:, bass.ds(q * (CHUNK * D) + j * D, D)]
                                dve.scalar_tensor_tensor(at, nrows[:, s, j, :], scale[:, 1, bass.ds(q * CHUNK + j, 1)],
                                                         at, ALU.mult, ALU.add).then_inc(rows_added[r], 1)
                            if r == 1:
                                dve.wait_ge(rows_added[r], q * CHUNK + CHUNK)
                                stats_of(1, q, s, first)
                                invert(1, q, s, first)
                        else:
                            if r == 3:
                                dve.wait_ge(root_sb[2], q + 1)
                            elif first and s == 0:
                                dve.wait_ge(root_sb[1], CHUNKS)
                            for j in range(CHUNK):
                                dve.scalar_tensor_tensor(nrows[:, s, j, :], nrows[:, s, j, :],
                                                         scale[:, 2, bass.ds(q * CHUNK + j, 1)],
                                                         root[:, bass.ds(q * (CHUNK * D) + j * D, D)],
                                                         ALU.mult, ALU.add).then_inc(rows_added[r], 1)
                            dve.wait_ge(rows_added[r], q * CHUNK + CHUNK)
                            if r == 2 and not first:
                                dve.wait_ge(ht_ps[2], q - 1)
                            v = nrows[:, s].rearrange("p t d -> p (t d)")
                            h = hbuf[:, s].rearrange("p t d -> p (t d)")
                            if r == 3 and not first:
                                dve.wait_ge(out_ready, q - 1)
                            m = dve.scalar_tensor_tensor(h, v, SLOPE, v, ALU.mult, ALU.max)
                            m.then_inc(act_done[r], 1)
                            if r == 3:
                                dve.wait_ge(act_done[3], q + 1)
                                dve.tensor_tensor(xs[:, here], xs[:, here], h, ALU.add).then_inc(out_ready, 1)

                node(0, True)
                with dve.Fori(1, CPAIRS) as i:
                    node(i, False)


_INS = ["x", "src", "dst", "eat", "eat_tail", "W1_msg", "W1_edge", "W1_root", "b1",
        "W2_msg", "W2_edge", "W2_root", "b2"]


def kernel(x, src, dst, edge_attr_32, L1_gnn_W1_msg, L1_gnn_W1_edge, L1_gnn_W1_root, L1_gnn_b1,
           L1_gnn_W2_msg, L1_gnn_W2_edge, L1_gnn_W2_root, L1_gnn_b2):
    import concourse.bacc as bacc
    from concourse.bass_utils import run_bass_kernel_spmd as run

    ea = np.ascontiguousarray(edge_attr_32)
    lo = ea[:REST * SHARE].reshape(REST, SHARE, DE).transpose(2, 1, 0)
    hi = ea[REST * SHARE:].reshape(P - REST, COLS, DE).transpose(2, 1, 0)
    eat = np.concatenate([lo[:, :COLS], hi], axis=2).reshape(DE, COLS * P)
    eat_tail = np.ascontiguousarray(lo[:, COLS])
    values = [x, src, dst, eat, eat_tail, L1_gnn_W1_msg, L1_gnn_W1_edge, L1_gnn_W1_root, L1_gnn_b1,
              L1_gnn_W2_msg, L1_gnn_W2_edge, L1_gnn_W2_root, L1_gnn_b2]
    nc = bacc.Bacc("TRN2", target_bir_lowering=False, num_devices=1)
    arrays, args = {}, []
    for name, value in zip(_INS, values):
        a = np.ascontiguousarray(value)
        arrays[f"in_{name}"] = a
        args.append(nc.dram_tensor(f"in_{name}", a.shape, mybir.dt.from_np(a.dtype), kind="ExternalInput").ap())
    args.append(nc.dram_tensor("out_0", (N, D), F32, kind="ExternalOutput").ap())
    gnn(nc, *args)
    r = run(nc, [arrays], core_ids=[0])
    return r.results[0]["out_0"]
```

```python
from contextlib import ExitStack

import numpy as np

import concourse.bass as bass
from concourse import mybir

F32 = mybir.dt.float32
BF16 = mybir.dt.bfloat16
I32 = mybir.dt.int32
U32 = mybir.dt.uint32
ALU = mybir.AluOpType
ACT = mybir.ActivationFunctionType

P = 128
N, D = 12500, 96
E, DE = 200000, 32
BATCHES = E // P
REST = E - P * BATCHES
COLS = BATCHES + 1
UNIT = 11
UNITS = BATCHES // UNIT
PAIRS = UNITS // 2
GROUPS = (4, 4, 3)
G = len(GROUPS)
TILES = -(-N // P)
LEFT = N - (TILES - 1) * P
CHUNK = 7
CHUNKS = TILES // CHUNK
NPAD = P * TILES
X = D + 2
WIDE = NPAD + P
BIG = float(np.finfo(np.float32).max)
EPS = 1e-5
SLOPE = 0.01
ROUNDS = 4
ARENA = 10112
BANK = 512
PREP_START = 3
PREP_ALL = 17
PREP_MAX = 23
assert UNIT * UNITS == BATCHES and UNITS % 2 == 0 and CHUNK * CHUNKS == TILES and CHUNKS % 2 == 0
assert sum(GROUPS) == UNIT and (G * 2) % 2 == 0 and REST == 64


def known(q):
    return isinstance(q, int)


def after(q, n):
    return q >= n if known(q) else True


def pipeline(engine, body, lag):
    first = 2 + lag + (2 + lag) % 2
    pairs = (CHUNKS - first - 1) // 2
    for k in range(first):
        body(k, k % 2)
    with engine.Fori(0, pairs) as i:
        for s in range(2):
            body(i * 2 + (first + s), s)
    for k in range(first + 2 * pairs, CHUNKS + lag):
        body(k, k % 2)


def has(k, lag):
    return 0 <= k - lag < CHUNKS if known(k) else True


def gnn(nc, x, srcs, cur, prev, nxt, eat, wm1, we1, wr1, b1, wm2, we2, wr2, b2, out):
    with ExitStack() as ctx:
        def sb(name, shape, dt=F32):
            return ctx.enter_context(nc.sbuf_tensor(name, shape, dt))

        def sem(name):
            return ctx.enter_context(nc.semaphore(name))

        def sems(name, of, slots=0):
            one = (lambda n: [sem(f"{n}_slot{s}") for s in range(slots)]) if slots else sem
            return {k: one(f"{name}_{k}") for k in of}

        tables = [nc.dram_tensor(f"table{r}", (NPAD, D), F32).ap() for r in range(ROUNDS)]

        comp = sb("comp", [X, WIDE])
        xs = sb("xs", [P, TILES * D])
        root = sb("root", [P, TILES * D])
        part = [root[:, k * COLS:(k + 1) * COLS] for k in range(6)]
        cur_i, prev_i, next_i = (part[k].bitcast(I32) for k in range(3))
        hi_i, relf = prev_i, part[1]
        node1, startf, endf = part[3:6]

        src_sb = sb("src_sb", [P, COLS], I32)
        meta = sb("meta", [P, UNITS, 4, UNIT], BF16)
        meta_t = sb("meta_t", [P, 4])
        start_b = sb("start_b", [P, COLS], BF16)
        base = sb("base", [1, COLS], I32)
        node_base = sb("node_base", [1, TILES], I32)
        base_f = sb("base_f", [1, TILES])

        idx_u = sb("idx_u", [P, 2, UNIT], U32)
        meta_u = sb("meta_u", [P, 2, 2, UNIT])
        bit_u = sb("bit_u", [P, 2, UNIT], BF16)
        rows_u = sb("rows_u", [P, 2, UNIT, X])
        idx_t = sb("idx_t", [P, 1], U32)
        bit_t = sb("bit_t", [P, 1], BF16)
        cont_t = sb("cont_t", [P, 1], BF16)
        rows_t = sb("rows_t", [P, X])

        arena = sb("arena", [P, ARENA])

        def carve(at, shape, dt=F32, parts=P):
            n = int(np.prod(shape[1:]))
            w = n if dt == F32 else n // 2
            v = arena[0:parts, at:at + w]
            v = v if dt == F32 else v.bitcast(dt)
            names = "abcd"[:len(shape) - 1]
            if len(names) > 1:
                v = v.rearrange(f"p ({' '.join(names)}) -> p {' '.join(names)}",
                                **{c: m for c, m in zip(names, shape[1:])})
            return v, at + w

        hot_u, at = carve(0, [P, 2, UNIT, P])
        hot_t, at = carve(at, [P, P])
        eat_u, at = carve(at, [DE, 2, UNIT * P], parts=DE)
        eat_t, at = carve(at, [DE, REST], parts=DE)
        run_g, at2 = carve(at, [D, 2, 4 * P], parts=D)
        flag_g, at2 = carve(at2, [D, 2, 4 * P], parts=D)
        runT_g, at2 = carve(at2, [P, 2, 4, D])
        tile_u, at3 = carve(at, [P, 2, UNIT, TILES], BF16)
        tile_t, at3 = carve(at3, [P, TILES], BF16)
        assert max(at2, at3) <= ARENA
        win_c, at = carve(0, [P, 2, CHUNK, X])
        spread_c, at = carve(at, [P, 2, CHUNK, P])
        hbuf, at = carve(at, [P, 2, CHUNK, D])
        nout, at = carve(at, [P, 2, CHUNK, D])
        hT, at = carve(at, [D + 1, 2, CHUNK * P], parts=D + 1)
        tmp, at = carve(at, [P, CHUNK, D])
        win_f, at = carve(at, [X, 2, CHUNK, P], parts=X)
        assert at <= ARENA

        scale = sb("scale", [P, TILES])
        rel_c = sb("rel_c", [P, 2, CHUNK])
        node_rel = sb("node_rel", [P, TILES])
        tile_at = sb("tile_at", [P, TILES])
        stats = sb("stats", [P, 2, CHUNK, 6])
        mv = sb("mv", [P, 2, CHUNK, 2])
        std = sb("std", [P, 2, CHUNK])
        rstd = sb("rstd", [P, 2, CHUNK])
        nbias = sb("nbias", [P, 2, CHUNK])
        eps = sb("eps", [P, 1])
        ident = sb("ident", [P, P])
        ident_b = sb("ident_b", [P, P], BF16)
        upto_b = sb("upto_b", [P, P], BF16)
        ones_b = sb("ones_b", [P, 1], BF16)
        iota_0 = sb("iota_0", [P, P])
        iota_1 = sb("iota_1", [P, P])
        iota_b = sb("iota_b", [P, TILES], BF16)
        wcat = sb("wcat", [D + 1, 2, 2 * D])
        we = sb("we", [DE, 2, D])

        ps = ctx.enter_context(nc.psum_tensor("ps", [P, 8 * BANK], F32))
        WIN, ROWS, FLAG, RUNT, COUNT = 0, 2 * BANK, 4 * BANK, 6 * BANK, 2 * BANK
        TRANS, PROD = 2 * BANK, 4 * BANK
        SPREAD = {0: (4 * BANK, 6 * BANK), 1: (0, 0), 2: (0, 0), 3: (4 * BANK, 6 * BANK)}
        LAG_SPREAD = {0: 1, 1: 0, 2: 0, 3: 1}
        LAG_PROD = {1: 2, 2: 2}
        LAGS = {0: 1, 1: 3, 2: 3, 3: 1}
        POOL_HOTS = {0: 2, 1: 7, 2: 5, 3: 4}


        rounds, sums, maxima, projected = range(ROUNDS), (0, 1), (2, 3), (1, 2)
        s_dst, s_next, s_src, s_w = sem("dst_in"), sem("next_dst_in"), sem("src_in"), sem("weights_in")
        s_tail = sem("tail_edge_features_in")
        s_x = sems("x_in", range(CHUNKS // 2))
        const, xpad = sem("constants_made"), sem("x_padding_made")
        pool_go, dve_go = sem("pool_goes_on"), sem("dve_goes_on")
        prep, dveinit, cleared = sem("prep_steps"), sem("dve_init"), sem("comp_cleared")
        ranked = sem("ranks_in_psum")
        idx_ready, meta_ready = sems("idx_ready", rounds), sems("meta_ready", rounds)
        landed = {r: [[sem(f"rows_landed_{r}_slot{s}_group{b}") for b in range(G)] for s in range(2)] for r in rounds}
        tail_idx = sem("tail_idx_ready")
        tail_rows = sems("tail_rows_landed", rounds)
        eat_in = sems("edge_features_in", maxima, 2)
        hot_ready, picked = sems("onehots_ready", rounds), sems("window_ready", rounds)
        folded = sems("window_in_comp", rounds)
        tile_ready, counted = sem("tile_onehots_ready"), sem("segments_counted")
        count_steps = sem("count_steps")
        flags_ps, flags_sb = sems("flags_in_psum", maxima), sems("flags_in_sbuf", maxima)
        rows_ps, scanned = sems("rows_in_psum", maxima), sems("scanned", maxima)
        runT_ps, runT_sb = sems("running_transposed", maxima), sems("running_in_sbuf", maxima)
        wins = sems("windows_copied", rounds)
        win_ps, win_sb = sems("windows_transposed", rounds), sems("windows_in_sbuf", rounds)
        spread_1h, spread_ps = sems("spread_onehots_of_pool", rounds), sems("nodes_in_psum", rounds)
        spread_1h_dve = sems("spread_onehots_of_dve", [r for r in rounds if POOL_HOTS[r] < CHUNK])
        rel_ready, stepA = sems("node_rel_ready", rounds), sems("node_steps", rounds)
        stats_done, aggr_done, std_done = (sems(n, (0, 1)) for n in ("stats_done", "aggr_done", "std_done"))
        rstd_done, nbias_done, normed = (sems(n, (0, 1)) for n in ("rstd_done", "nbias_done", "normed"))
        ht_ps, ht_sb = sems("transposed", projected), sems("transposes_copied", projected)
        prod, root_sb = sems("products_ready", projected), sems("root_ready", projected)
        out_sb = sems("table_rows_ready", projected)
        tstored = sems("table_stored", rounds, 2)
        out_stored = sem("output_stored")
        STEPS = {0: 4, 1: 2, 2: 2, 3: 3}
        READ = {0: 3, 1: 1, 2: 1, 3: 1}

        def table_view(t, q):
            return t[bass.ds(q * (CHUNK * P), CHUNK * P), :].rearrange("(t p) d -> p t d", p=P)

        def chunk(buffer, q):
            return buffer[:, bass.ds(q * (CHUNK * D), CHUNK * D)].rearrange("p (t d) -> p t d", t=CHUNK)

        def groups(unit_slot):
            first = 0
            for b, n in enumerate(GROUPS):
                yield b, n, first, (G * unit_slot + b) % 2
                first += n

        def unit_pairs(engine, body):
            body(0, True, False)
            with engine.Fori(1, PAIRS - 1) as i:
                body(i, False, False)
            body(PAIRS - 1, False, True)

        def numbers(engine, ap):
            return nc.values_load_multi_w_load_instructions(
                ap, engines=[engine], min_val=0, max_val=NPAD,
                skip_runtime_bounds_check_because="ranks are below the count of nodes")[1]

        block = ctx.enter_context(nc.Block())

        @block.sync
        def _(sp):
            sp.wait_ge(xpad, 1)
            def load_x(g):
                t0, t1 = 2 * CHUNK * g, min(2 * CHUNK * (g + 1), TILES - 1)
                sp.dma_start(xs[:, t0 * D:t1 * D].rearrange("p (t d) -> p t d", d=D),
                             x[t0 * P:t1 * P, :].rearrange("(t p) d -> p t d", p=P)).then_inc(s_x[g], 16)
                if t1 == TILES - 1:
                    sp.dma_start(xs[0:LEFT, t1 * D:], x[t1 * P:N, :]).then_inc(s_x[g], 16)

            for g in range(3):
                load_x(g)
            for q in range(CHUNKS):
                sp.wait_ge(normed[0], q + 1)
                sp.dma_start(table_view(tables[0], q), hbuf[:, q % 2]).then_inc(tstored[0][q % 2], 16)
                if q % 2 == 0 and 3 + q // 2 < CHUNKS // 2:
                    load_x(3 + q // 2)
                elif q == 8:
                    sp.dma_start(src_sb[:, :], srcs).then_inc(s_src, 16)
                elif q == 9:
                    sp.dma_start(cur_i, cur).then_inc(s_dst, 16)
                elif q == 10:
                    sp.dma_start(prev_i, prev).then_inc(s_dst, 16)
            sp.dma_start(next_i, nxt).then_inc(s_next, 16)

            for r in (0, 1, 2):
                with sp.Fori(0, CHUNKS // 2) as i:
                    for s in range(2):
                        if r == 0:
                            sp.wait_ge(stepA[0], (i * 2 + s) * STEPS[0] + READ[0])
                        else:
                            sp.wait_ge(out_sb[r], i * 2 + (s + 1))
                        sp.dma_start(table_view(tables[r + 1], i * 2 + s), nout[:, s]).then_inc(tstored[r + 1][s], 16)
            with sp.Fori(0, CHUNKS - 1) as q:
                sp.wait_ge(stepA[3], q * STEPS[3] + STEPS[3])
                sp.dma_start(table_view(out, q), chunk(xs, q)).then_inc(out_stored, 16)
            sp.wait_ge(stepA[3], CHUNKS * STEPS[3])
            t0 = TILES - CHUNK
            sp.dma_start(out[t0 * P:(TILES - 1) * P, :].rearrange("(t p) d -> p t d", p=P),
                         xs[:, t0 * D:(TILES - 1) * D].rearrange("p (t d) -> p t d", d=D)).then_inc(out_stored, 16)
            sp.dma_start(out[(TILES - 1) * P:N, :], xs[0:LEFT, (TILES - 1) * D:]).then_inc(out_stored, 16)
            sp.wait_ge(out_stored, 16 * (CHUNKS + 1))

        @block.gpsimd
        def _(pool):
            pool.memset(ident[:], 0.0).then_inc(const, 1)
            pool.memset(ident_b[:], 0.0).then_inc(const, 1)
            pool.memset(upto_b[:], 1.0).then_inc(const, 1)
            pool.memset(ones_b[:], 1.0).then_inc(const, 1)
            pool.wait_ge(const, 4)
            for eye in (ident, ident_b):
                pool.affine_select(out=eye[:], in_=eye[:], compare_op=ALU.not_equal, fill=1.0, base=0,
                                   pattern=[[-1, P]], channel_multiplier=1).then_inc(const, 1)
            pool.affine_select(out=upto_b[:], in_=upto_b[:], compare_op=ALU.is_ge, fill=0.0, base=0,
                               pattern=[[1, P]], channel_multiplier=-1).then_inc(const, 1)
            pool.wait_ge(const, 7)
            pool.affine_select(out=upto_b[:], in_=upto_b[:], compare_op=ALU.is_gt, fill=0.0, base=0,
                               pattern=[[0, P]], channel_multiplier=1).then_inc(const, 1)
            for to, w, step, first in ((iota_0, P, 1, 0), (iota_1, P, 1, 1), (iota_b, TILES, 1, 0), (tile_at, TILES, P, 0)):
                pool.iota(to[:], pattern=[[step, w]], base=first, channel_multiplier=0,
                          allow_small_or_imprecise_dtypes=True).then_inc(const, 1)
            pool.memset(comp[:], 0.0).then_inc(cleared, 1)

            def gather(r, to, idx):
                return pool.indirect_dma_start(to, None, tables[r][:, :], bass.IndirectOffsetOnAxis(idx, 0))

            for r in range(ROUNDS):
                for s in range(2):
                    pool.wait_ge(tstored[r][s], 16 * (CHUNKS // 2))
                used = picked[r] if r in sums else rows_ps[r]

                def pair(i, first, last):
                    for s in range(2):
                        pool.wait_ge(idx_ready[r], i * 2 + (s + 1))
                        if not first:
                            pool.wait_ge(used, (i - 1) * (2 * G) + G * (s + 1))
                        pool.sem_inc(pool_go, 1)
                        for b, n, first_batch, _ in groups(s):
                            for c in range(first_batch, first_batch + n):
                                gather(r, rows_u[:, s, c, 0:D], idx_u[:, s, c:c + 1]).then_inc(landed[r][s][b], 16)

                unit_pairs(pool, pair)
                if r == 0:
                    pool.wait_ge(tail_idx, 1)
                gather(r, rows_t[0:REST, 0:D], idx_t[0:REST, :]).then_inc(tail_rows[r], 16)

                pool.wait_ge(folded[r], COLS)

                def spread(k, s):
                    if not has(k, 0):
                        return
                    pool.wait_ge(rel_ready[r], k + 1)
                    if after(k, 2):
                        pool.wait_ge(spread_ps[r], k - 1)
                    pool.sem_inc(pool_go, 1)
                    for j in range(POOL_HOTS[r]):
                        pool.tensor_scalar(spread_c[:, s, j, :], iota_1[:, :], rel_c[:, s, j:j + 1],
                                           None, ALU.is_equal).then_inc(spread_1h[r], 1)

                pipeline(pool, spread, 0)

        @block.scalar
        def _(act):
            act.wait_ge(dveinit, 1)
            for k, (wm, wr, b, wed) in enumerate(((wm1, wr1, b1, we1), (wm2, wr2, b2, we2))):
                act.dma_start(wcat[0:D, k, 0:D], wm).then_inc(s_w, 16)
                act.dma_start(wcat[0:D, k, D:2 * D], wr).then_inc(s_w, 16)
                act.dma_start(wcat[D:D + 1, k, D:2 * D], b.rearrange("(a d) -> a d", a=1)).then_inc(s_w, 16)
                act.dma_start(we[:, k, :], wed).then_inc(s_w, 16)

            def deviation(k, q, s):
                act.wait_ge(aggr_done[k], q * CHUNK + CHUNK)
                if after(q, 2):
                    act.wait_ge(rstd_done[k], q - 1)
                act.activation(std[:, s], mv[:, s, :, 1], ACT.Sqrt, bias=eps[:, 0:1]).then_inc(std_done[k], 1)

            def norm(k, q, s):
                act.wait_ge(nbias_done[k], q + 1)
                if after(q, 2):
                    if k == 0:
                        act.wait_ge(tstored[0][s], (q // 2) * 16)
                    else:
                        act.wait_ge(ht_ps[1], q - 1)
                for j in range(CHUNK):
                    m = act.activation(hbuf[:, s, j, :], xs[:, bass.ds(q * (CHUNK * D) + j * D, D)], ACT.Relu,
                                       bias=nbias[:, s, j:j + 1], scale=rstd[:, s, j:j + 1])
                m.then_inc(normed[k], 1)

            for q in range(CHUNKS + 1):
                if q < CHUNKS:
                    deviation(0, q, q % 2)
                if q:
                    norm(0, q - 1, (q - 1) % 2)
            act.wait_ge(s_src, 16)
            act.copy(idx_t[0:REST, :], src_sb[0:REST, BATCHES:COLS]).then_inc(tail_idx, 1)

            for r in range(ROUNDS):
                def stage_idx(u, s):
                    act.copy(idx_u[:, s, :], src_sb[:, bass.ds(u * UNIT, UNIT)]).then_inc(idx_ready[r], 1)

                def stage_meta(u, s, again):
                    at = bass.ds(u, 1)
                    if again:
                        act.wait_ge(hot_ready[r], (u - 1) * UNIT)
                        act.wait_ge(picked[r] if r in sums else rows_ps[r], (u - 1) * G)
                        if r == 0:
                            act.wait_ge(counted, u - 1)
                    if r == 0:
                        act.copy(meta_u[:, s], meta[:, at, 0:2, :]).then_inc(meta_ready[r], 1)
                        act.copy(bit_u[:, s], start_b[:, bass.ds(u * UNIT, UNIT)]).then_inc(meta_ready[r], 1)
                        act.copy(rows_u[:, s, :, D + 1], node1[:, bass.ds(u * UNIT, UNIT)]).then_inc(meta_ready[r], 1)
                    elif r == 1:
                        act.copy(meta_u[:, s, 0, :], meta[:, at, 0, :]).then_inc(meta_ready[r], 1)
                    else:
                        act.copy(meta_u[:, s, 0, :], meta[:, at, 2, :]).then_inc(meta_ready[r], 1)
                        act.copy(bit_u[:, s], meta[:, at, 3, :]).then_inc(meta_ready[r], 1)
                        act.dma_start(eat_u[:, s], eat[:, bass.ds(u * (UNIT * P), UNIT * P)]).then_inc(eat_in[r][s], 16)

                stage_idx(0, 0)
                stage_idx(1, 1)
                if r in (0, 2):
                    act.wait_ge(prep, PREP_MAX if r else PREP_ALL)
                for s in range(2):
                    act.wait_ge(tstored[r][s], 16 * (CHUNKS // 2))
                stage_meta(0, 0, False)
                if r in maxima:
                    act.dma_start(eat_t[:, :], eat[:, BATCHES * P:E]).then_inc(s_tail, 16)

                def copy_flags(g, gs, n, w=P):
                    act.wait_ge(flags_ps[r], g + 1)
                    if after(g, 2):
                        act.wait_ge(scanned[r], g - 1)
                    act.activation(flag_g[:, gs, 0:n * w], ps[0:D, FLAG + gs * BANK:FLAG + gs * BANK + n * w],
                                   ACT.Copy, scale=BIG).then_inc(flags_sb[r], 1)

                def copy_running(g, gs, n, edges=P):
                    act.wait_ge(runT_ps[r], g + 1)
                    if after(g, 2):
                        act.wait_ge(picked[r], g - 1)
                    act.copy(runT_g[0:edges, gs, 0:n, :].rearrange("p k d -> p (k d)"),
                             ps[0:edges, RUNT + gs * BANK:RUNT + gs * BANK + n * D]).then_inc(runT_sb[r], 1)

                def windows(g, gs, n, batch):
                    act.wait_ge(picked[r], g + 1)
                    for j, at in enumerate(numbers(act.engine, base[0:1, bass.ds(batch, n)])):
                        if not (known(batch) and batch == 0 and j == 0):
                            act.wait_ge(folded[r], batch + j)
                        act.copy(comp[0:D, bass.ds(at, P)], ps[0:D, WIN + gs * BANK + j * P:WIN + gs * BANK + (j + 1) * P]
                                 ).then_inc(folded[r], 1)

                def pair(i, first, last):
                    for s in range(2):
                        u = i * 2 + s

                        if r in sums and not (last and s == 1):
                            stage_meta(u + 1, 1 - s, not (first and s == 0))
                        for b, n, c, gs in groups(s) if r in maxima else ():
                            g = i * (2 * G) + (G * s + b)
                            done = first and s == 0
                            if not (done and b == 0):
                                copy_running(g - 1, 1 - gs, GROUPS[b - 1])
                            if last and s == 1 and b == G - 1:
                                copy_flags(g + 1, 1 - gs, 1, REST)
                            else:
                                copy_flags(g + 1, 1 - gs, GROUPS[(b + 1) % G])
                            if not (done and b < 2):
                                windows(g - 2, gs, GROUPS[b - 2], u * UNIT + (c - GROUPS[b - 1] - GROUPS[b - 2]))
                            if b == 0 and not (last and s == 1):
                                stage_meta(u + 1, 1 - s, not (first and s == 0))
                        if not last:
                            for b, n, _, _ in groups(s):
                                act.wait_ge(landed[r][s][b], i * (16 * n) + 16 * n)
                            stage_idx(u + 2, s)

                if r in maxima:
                    copy_flags(0, 0, GROUPS[0])
                unit_pairs(act, pair)
                if r in maxima:
                    g = G * UNITS
                    copy_running(g - 1, 1, GROUPS[-1])
                    windows(g - 2, 0, GROUPS[-2], BATCHES - GROUPS[-1] - GROUPS[-2])
                    copy_running(g, 0, 1, REST)
                    windows(g - 1, 1, GROUPS[-1], BATCHES - GROUPS[-1])
                    windows(g, 0, 1, BATCHES)

                act.wait_ge(folded[r], COLS)
                if r == 0:
                    act.wait_ge(count_steps, 3)

                def windows_of(k, s):
                    w = X if r == 0 else D
                    starts = numbers(act.engine, node_base[0:1, bass.ds(k * CHUNK, CHUNK)])
                    if after(k, 2):
                        act.wait_ge(win_ps[r], k - 1)
                    for j, at in enumerate(starts):
                        act.copy(win_f[0:w, s, j, :], comp[0:w, bass.ds(at, P)]).then_inc(wins[r], 1)

                def stage_rel(k, s):
                    if after(k, 2):
                        act.wait_ge(spread_1h[r], (k - 1) * POOL_HOTS[r])
                        if r in spread_1h_dve:
                            act.wait_ge(spread_1h_dve[r], (k - 1) * (CHUNK - POOL_HOTS[r]))
                    act.copy(rel_c[:, s], node_rel[:, bass.ds(k * CHUNK, CHUNK)]).then_inc(rel_ready[r], 1)

                def nodes(k, s):
                    if known(k) and k == 0:
                        if r:
                            stage_rel(0, 0)
                        windows_of(0, 0)
                    if has(k, 0):
                        act.wait_ge(win_ps[r], k + 1)
                        if after(k, 2):
                            act.wait_ge(spread_ps[r], k - 1)
                        w = X if r == 0 else D
                        act.copy(win_c[:, s, :, 0:w], ps[:, 0:CHUNK * P].rearrange("p (t c) -> p t c", c=P)[:, :, 0:w]
                                 ).then_inc(win_sb[r], 1)
                    if r in projected and has(k, LAG_PROD[r] + 1):
                        q, qs = k - LAG_PROD[r] - 1, (s + LAG_PROD[r] + 1) % 2
                        act.wait_ge(prod[r], q + 1)
                        if after(q, 2):
                            act.wait_ge(tstored[r + 1][qs], (q - qs) * 8)
                        pv = ps[:, PROD:PROD + CHUNK * 256].rearrange("p (t c) -> p t c", c=256)
                        act.copy(nout[:, qs], pv[:, :, 0:D]).then_inc(out_sb[r], 1)
                        rv = pv[:, :, D:2 * D]
                        if known(q) and q == CHUNKS - 1:
                            act.wait_ge(prod[r], CHUNKS + 1)
                            rv = ps[:, SPREAD[r][qs]:SPREAD[r][qs] + CHUNK * P].rearrange("p (t c) -> p t c", c=P)[:, :, 0:D]
                        act.copy(chunk(root, q), rv).then_inc(root_sb[r], 1)
                    if r == 1 and has(k, 1):
                        deviation(1, k - 1, 1 - s)
                    if not known(k) or k + 1 < CHUNKS:
                        if r:
                            stage_rel(k + 1, 1 - s)
                        windows_of(k + 1, 1 - s)
                    if r == 1 and has(k, 1):
                        norm(1, k - 1, 1 - s)

                pipeline(act, nodes, LAGS[r])

        @block.tensor
        def _(pe):
            pe.wait_ge(const, 12)
            pe.wait_ge(prep, PREP_START)
            for a in range(0, COLS, BANK):
                b = min(a + BANK, COLS)
                pe.matmul(ps[:, a:b], upto_b[:, :], start_b[:, a:b], start=True, stop=True)
            for a in range(0, COLS, BANK):
                b = min(a + BANK, COLS)
                m = pe.matmul(ps[0:1, 4 * BANK + a:4 * BANK + b], ones_b[:, :], start_b[:, a:b], start=True, stop=True)
            m.then_inc(ranked, 1)

            for r in range(ROUNDS):
                if r in sums:
                    w = X if r == 0 else D

                    def pair(i, first, last):
                        for s in range(2):
                            u = i * 2 + s
                            pe.wait_ge(hot_ready[r], u * UNIT + UNIT)
                            if r == 0:
                                pe.wait_ge(meta_ready[0], u * 3 + 3)
                            for b, n, c, gs in groups(s):
                                g = i * (2 * G) + (G * s + b)
                                pe.wait_ge(landed[r][s][b], i * (16 * n) + 16 * n)
                                if not (first and s == 0 and b < 2):
                                    pe.wait_ge(folded[r], u * UNIT + c - (GROUPS[b - 1] if b else GROUPS[-1]))
                                for j in range(n):
                                    m = pe.matmul(ps[0:w, WIN + gs * BANK + j * P:WIN + gs * BANK + (j + 1) * P],
                                                  rows_u[:, s, c + j, 0:w], hot_u[:, s, c + j, :], start=True, stop=True)
                                m.then_inc(picked[r], 1)
                            if r == 0:
                                pe.wait_ge(tile_ready, u * UNIT + UNIT)
                                for c in range(UNIT):
                                    m = pe.matmul(ps[0:1, COUNT:COUNT + TILES], bit_u[:, s, c:c + 1], tile_u[:, s, c, :],
                                                  start=(first and s == 0 and c == 0), stop=False, skip_group_check=True)
                                m.then_inc(counted, 1)

                    pe.wait_ge(prep, PREP_ALL)
                    unit_pairs(pe, pair)
                    pe.wait_ge(hot_ready[r], COLS)
                    pe.wait_ge(tail_rows[r], 16)
                    pe.wait_ge(folded[r], BATCHES - GROUPS[-1])
                    pe.matmul(ps[0:w, WIN:WIN + P], rows_t[0:REST, 0:w], hot_t[0:REST, :],
                              start=True, stop=True).then_inc(picked[r], 1)
                    if r == 0:
                        pe.wait_ge(tile_ready, COLS)
                        pe.matmul(ps[0:1, COUNT:COUNT + TILES], bit_t[0:REST, :], tile_t[0:REST, :],
                                  start=False, stop=True, skip_group_check=True).then_inc(counted, 1)
                else:
                    k = r - 2
                    if r == 2:
                        pe.wait_ge(s_w, 16 * 8)

                    def flags_of(g, gs, bits, w=P):
                        if after(g, 2):
                            pe.wait_ge(flags_sb[r], g - 1)
                        at = FLAG + gs * BANK
                        for j, bit in enumerate(bits):
                            m = pe.matmul(ps[0:D, at + j * w:at + (j + 1) * w], bit.to_broadcast([w, D]),
                                          ident_b[0:w, 0:w], start=True, stop=True)
                        m.then_inc(flags_ps[r], 1)

                    def unit_flags(g, gs, s, b):
                        c = sum(GROUPS[0:b])
                        flags_of(g, gs, [bit_u[:, s, c + j:c + j + 1] for j in range(GROUPS[b])])

                    def rows_of(g, gs, n, feats, rows, w=P):
                        if after(g, 2):
                            pe.wait_ge(scanned[r], g - 1)
                        at = ROWS + gs * BANK
                        pe.matmul(ps[0:D, at:at + n * w], we[:, k, :], feats, start=True, stop=False)
                        for j in range(n):
                            m = pe.matmul(ps[0:D, at + j * w:at + (j + 1) * w], rows[j], ident[0:w, 0:w],
                                          start=False, stop=(j == n - 1))
                        m.then_inc(rows_ps[r], 1)

                    def back(g, gs, n, w=P):
                        pe.wait_ge(scanned[r], g + 1)
                        if after(g, 2):
                            pe.wait_ge(runT_sb[r], g - 1)
                        for j in range(n):
                            m = pe.transpose(ps[0:w, RUNT + gs * BANK + j * D:RUNT + gs * BANK + (j + 1) * D],
                                             run_g[:, gs, j * w:(j + 1) * w], ident[0:D, 0:D])
                        m.then_inc(runT_ps[r], 1)

                    def pick(g, gs, n, hots, done, w=P):
                        pe.wait_ge(runT_sb[r], g + 1)
                        if after(g, 2):
                            pe.wait_ge(folded[r], done)
                        for j in range(n):
                            m = pe.matmul(ps[0:D, WIN + gs * BANK + j * P:WIN + gs * BANK + (j + 1) * P],
                                          runT_g[0:w, gs, j, :], hots[j], start=True, stop=True)
                        m.then_inc(picked[r], 1)

                    def pair(i, first, last):
                        for s in range(2):
                            u = i * 2 + s
                            for b, n, c, gs in groups(s):
                                g = i * (2 * G) + (G * s + b)
                                start = first and s == 0 and b == 0
                                bn = GROUPS[b - 1]
                                bs, bc = (s, c - bn) if b else (1 - s, UNIT - bn)
                                bdone = u * UNIT + c - bn - GROUPS[b - 2]
                                if not start:
                                    back(g - 1, 1 - gs, bn)
                                if b == 0:
                                    pe.wait_ge(eat_in[r][s], i * 16 + 16)
                                pe.wait_ge(landed[r][s][b], i * (16 * n) + 16 * n)
                                rows_of(g, gs, n, eat_u[:, s, c * P:(c + n) * P],
                                        [rows_u[:, s, c + j, 0:D] for j in range(n)])
                                if b < G - 1:
                                    unit_flags(g + 1, 1 - gs, s, b + 1)
                                elif not (last and s == 1):
                                    pe.wait_ge(meta_ready[r], u * 2 + 4)
                                    unit_flags(g + 1, 1 - gs, 1 - s, 0)
                                else:
                                    flags_of(g + 1, 1 - gs, [cont_t[0:REST, :]], REST)
                                if not start:
                                    if b <= 1:
                                        pe.wait_ge(hot_ready[r], u * UNIT + (UNIT if b else 0))
                                    pick(g - 1, 1 - gs, bn, [hot_u[:, bs, bc + j, :] for j in range(bn)], bdone)

                    pe.wait_ge(meta_ready[r], 2)
                    unit_flags(0, 0, 0, 0)
                    unit_pairs(pe, pair)
                    g, n = G * UNITS, GROUPS[-1]
                    back(g - 1, 1, n)
                    pe.wait_ge(tail_rows[r], 16)
                    pe.wait_ge(s_tail, 16 * (r - 1))
                    rows_of(g, 0, 1, eat_t[:, :], [rows_t[0:REST, 0:D]], REST)
                    pick(g - 1, 1, n, [hot_u[:, 1, UNIT - n + j, :] for j in range(n)], BATCHES - n - GROUPS[-2])
                    back(g, 0, 1, REST)
                    pe.wait_ge(hot_ready[r], COLS)
                    pick(g, 0, 1, [hot_t[0:REST, :]], BATCHES - n, REST)

                pe.wait_ge(folded[r], COLS)
                w = X if r == 0 else D
                lag = LAG_SPREAD[r]

                def nodes(k, s):
                    if has(k, 0):
                        pe.wait_ge(wins[r], k * CHUNK + CHUNK)
                        if after(k, 1):
                            pe.wait_ge(win_sb[r], k)
                            if lag == 0:
                                pe.wait_ge(stepA[r], (k - 1) * STEPS[r] + READ[r])
                        for j in range(CHUNK):
                            m = pe.transpose(ps[:, j * P:j * P + w], win_f[0:w, s, j, :], ident[0:w, 0:w])
                        m.then_inc(win_ps[r], 1)
                    if r in projected and has(k, LAG_PROD[r]):
                        q, qs = k - LAG_PROD[r], (s + LAG_PROD[r]) % 2
                        if r == 1:
                            pe.wait_ge(normed[1], q + 1)
                        else:
                            pe.wait_ge(stepA[2], q * STEPS[2] + STEPS[2])
                        if after(q, 1):
                            pe.wait_ge(ht_sb[r], q)
                        for j in range(CHUNK):
                            m = pe.transpose(ps[0:D, TRANS + j * P:TRANS + (j + 1) * P], hbuf[:, qs, j, :], ident[:, :])
                        m.then_inc(ht_ps[r], 1)
                    if has(k, lag):
                        q, qs = k - lag, (s + lag) % 2
                        pe.wait_ge(win_sb[r], q + 1)
                        pe.wait_ge(spread_1h[r], q * POOL_HOTS[r] + POOL_HOTS[r])
                        if r in spread_1h_dve:
                            pe.wait_ge(spread_1h_dve[r], q * (CHUNK - POOL_HOTS[r]) + (CHUNK - POOL_HOTS[r]))
                        if lag and after(q, 2):
                            pe.wait_ge(stepA[r], (q - 2) * STEPS[r] + READ[r])
                        at_spread = SPREAD[r][qs]
                        for j in range(CHUNK):
                            m = pe.matmul(ps[:, at_spread + j * P:at_spread + j * P + w], spread_c[:, qs, j, :],
                                          win_c[:, qs, j, 0:w], start=True, stop=True)
                        m.then_inc(spread_ps[r], 1)
                    if r in projected and has(k, LAG_PROD[r]):
                        q, qs = k - LAG_PROD[r], (s + LAG_PROD[r]) % 2
                        pe.wait_ge(ht_sb[r], q + 1)
                        if after(q, 1):
                            pe.wait_ge(root_sb[r], q)
                        elif r == 1:
                            pe.wait_ge(s_w, 16 * 8)
                        last = known(q) and q == CHUNKS - 1
                        cols = D if last else 2 * D
                        for j in range(CHUNK):
                            m = pe.matmul(ps[:, PROD + 256 * j:PROD + 256 * j + cols], hT[:, qs, j * P:(j + 1) * P],
                                          wcat[:, r - 1, 0:cols], start=True, stop=True)
                        m.then_inc(prod[r], 1)
                        if last:
                            pe.wait_ge(stepA[r], q * STEPS[r] + READ[r])
                            at_spread = SPREAD[r][qs]
                            for j in range(CHUNK):
                                m = pe.matmul(ps[:, at_spread + j * P:at_spread + j * P + D], hT[:, qs, j * P:(j + 1) * P],
                                              wcat[:, r - 1, D:2 * D], start=True, stop=True)
                            m.then_inc(prod[r], 1)

                pipeline(pe, nodes, LAGS[r])

        @block.vector
        def _(dve):
            steps = [0]

            def step(ins):
                steps[0] += 1
                ins.then_inc(prep, 1)
                dve.wait_ge(prep, steps[0])

            def by_unit(v):
                return v[:, 0:BATCHES].rearrange("p (u k) -> p u k", k=UNIT)

            dve.memset(wcat[:], 0.0).then_inc(dveinit, 1)
            dve.memset(xs[LEFT // 32 * 32:P, (TILES - 1) * D:], 0.0).then_inc(xpad, 1)
            step(dve.memset(eps[:], EPS))

            def stats_of(k, q, s):
                if after(q, 2):
                    dve.wait_ge(nbias_done[k], q - 1)
                    dve.wait_ge(std_done[k], q - 1)
                dve.sem_inc(dve_go, 1)
                for j in range(CHUNK):
                    dve.bn_stats(stats[:, s, j, :], xs[:, bass.ds(q * (CHUNK * D) + j * D, D)]
                                 ).then_inc(stats_done[k], 1)
                dve.wait_ge(stats_done[k], q * CHUNK + CHUNK)
                dve.sem_inc(dve_go, 1)
                for j in range(CHUNK):
                    dve.bn_aggr(mv[:, s, j, :], stats[:, s, j, :]).then_inc(aggr_done[k], 1)

            def invert(k, q, s):
                dve.wait_ge(std_done[k], q + 1)
                if after(q, 2):
                    dve.wait_ge(normed[k], q - 1)
                dve.reciprocal(rstd[:, s], std[:, s]).then_inc(rstd_done[k], 1)
                dve.wait_ge(rstd_done[k], q + 1)
                dve.scalar_tensor_tensor(nbias[:, s], mv[:, s, :, 0], -1.0, rstd[:, s], ALU.mult,
                                         ALU.mult).then_inc(nbias_done[k], 1)

            for q in range(CHUNKS + 1):
                if q < CHUNKS:
                    if q % 2 == 0:
                        dve.wait_ge(s_x[q // 2], 32 if q == CHUNKS - 2 else 16)
                    stats_of(0, q, q % 2)
                if q:
                    invert(0, q - 1, (q - 1) % 2)

            dve.wait_ge(s_dst, 32)
            step(dve.tensor_tensor(startf, cur_i, prev_i, ALU.not_equal))
            step(dve.tensor_copy(start_b[:], startf))
            assert steps[0] == PREP_START
            step(dve.tensor_scalar(hi_i, cur_i, 7, None, ALU.arith_shift_right))
            step(dve.tensor_copy(meta[:, :, 1, :], by_unit(hi_i)))
            step(dve.tensor_copy(meta_t[:, 1:2], hi_i[:, BATCHES:]))
            dve.wait_ge(ranked, 1)
            step(dve.tensor_copy(relf, ps[:, 0:COLS]))
            step(dve.tensor_copy(meta[:, :, 0, :], by_unit(relf)))
            step(dve.tensor_copy(meta_t[:, 0:1], relf[:, BATCHES:]))
            incl = part[3][0:1]
            tot = ps[0:1, 4 * BANK:4 * BANK + COLS]
            dve.wait_ge(const, 12)
            step(dve.tensor_tensor_scan(incl, iota_1[0:1, 0:1].to_broadcast([1, COLS]), tot, 0.0, ALU.mult, ALU.add))
            step(dve.tensor_tensor(incl, incl, tot, ALU.subtract))
            step(dve.scalar_tensor_tensor(base[:], incl, -1.0, startf[0:1], ALU.add, ALU.add))
            step(dve.scalar_tensor_tensor(node1, cur_i, 1.0, startf, ALU.add, ALU.mult))
            step(dve.tensor_copy(rows_t[:, D + 1:X], node1[:, BATCHES:]))
            step(dve.memset(rows_t[:, D:D + 1], 1.0))
            step(dve.memset(rows_u[:, :, :, D], 1.0))
            step(dve.tensor_copy(bit_t[:], startf[:, BATCHES:]))
            assert steps[0] == PREP_ALL

            for r in range(ROUNDS):
                def hots(u, s, again, c0=0, c1=UNIT):
                    if c0 == 0:
                        per = {0: 3, 1: 1, 2: 2, 3: 2}[r]
                        dve.wait_ge(meta_ready[r], u * per + per)
                    if again and c0 == 0:
                        dve.wait_ge(picked[r], (u - 1) * G)
                        if r == 0:
                            dve.wait_ge(counted, u - 1)
                    for c in range(c0, c1):
                        dve.tensor_scalar(hot_u[:, s, c, :], iota_0[:, :], meta_u[:, s, 0, c:c + 1], None,
                                          ALU.is_equal).then_inc(hot_ready[r], 1)
                        if r == 0:
                            dve.tensor_scalar(tile_u[:, s, c, :], iota_b[:, :], meta_u[:, s, 1, c:c + 1], None,
                                              ALU.is_equal).then_inc(tile_ready, 1)

                def fold(batch, gs, n, w):
                    for j, at in enumerate(numbers(dve.engine, base[0:1, bass.ds(batch, n)])):
                        if not (known(batch) and batch + j == 0):
                            dve.wait_ge(folded[r], batch + j)
                        win = comp[0:w, bass.ds(at, P)]
                        dve.tensor_tensor(win, win, ps[0:w, WIN + gs * BANK + j * P:WIN + gs * BANK + (j + 1) * P],
                                          ALU.add).then_inc(folded[r], 1)

                for s in range(2):
                    dve.wait_ge(tstored[r][s], 16 * (CHUNKS // 2))
                hots(0, 0, False)
                if r == 0:
                    dve.wait_ge(s_next, 16)
                    step(dve.tensor_tensor(endf, cur_i, next_i, ALU.not_equal))
                    step(dve.tensor_tensor(relf, relf, endf, ALU.mult))
                    step(dve.scalar_tensor_tensor(relf, endf, -1.0, relf, ALU.add, ALU.add))
                    step(dve.tensor_copy(meta[:, :, 2, :], by_unit(relf)))
                    step(dve.tensor_copy(meta_t[:, 2:3], relf[:, BATCHES:]))
                    step(dve.tensor_scalar(meta[:, :, 3, :], by_unit(startf), -2.0, 1.0, ALU.mult, ALU.add))
                    dve.tensor_scalar(cont_t[:], startf[:, BATCHES:], -2.0, 1.0, ALU.mult, ALU.add).then_inc(dve_go, 1)
                    assert steps[0] == PREP_MAX
                    dve.wait_ge(cleared, 1)
                if r == 1:
                    dve.wait_ge(wins[0], TILES)
                    dve.memset(comp[0:D, :], 0.0).then_inc(cleared, 1)
                    dve.wait_ge(cleared, 2)

                def scan(g, gs, n, w=P):
                    dve.wait_ge(rows_ps[r], g + 1)
                    dve.wait_ge(flags_sb[r], g + 1)
                    if after(g, 2):
                        dve.wait_ge(runT_ps[r], g - 1)
                    if known(g) and g == 0:
                        initial = 0.0
                    else:
                        dve.wait_ge(scanned[r], g)
                        end = (GROUPS[-1] if w != P else prev_n) * P
                        initial = run_g[:, 1 - gs, end - 1:end]
                    dve.tensor_tensor_scan(run_g[:, gs, 0:n * w], flag_g[:, gs, 0:n * w],
                                           ps[0:D, ROWS + gs * BANK:ROWS + gs * BANK + n * w], initial,
                                           ALU.min, ALU.max).then_inc(scanned[r], 1)

                def pair(i, first, last):
                    nonlocal prev_n
                    for s in range(2):
                        u = i * 2 + s
                        for b, n, c, gs in groups(s):
                            g = i * (2 * G) + (G * s + b)
                            if r in sums:
                                dve.wait_ge(picked[r], g + 1)
                                fold(u * UNIT + c, gs, n, X if r == 0 else D)
                            else:
                                prev_n = GROUPS[b - 1]
                                scan(g, gs, n)
                            if b and not (last and s == 1):
                                cut = (UNIT + 1) // 2
                                hots(u + 1, 1 - s, not (first and s == 0), *((0, cut) if b == 1 else (cut, UNIT)))

                prev_n = 0
                unit_pairs(dve, pair)
                k = 0 if r in sums else 2
                if r == 0:
                    dve.tensor_scalar(tile_t[:, :], iota_b[:, :], meta_t[:, 1:2], None, ALU.is_equal).then_inc(tile_ready, 1)
                dve.tensor_scalar(hot_t[:, :], iota_0[:, :], meta_t[:, k:k + 1], None, ALU.is_equal).then_inc(hot_ready[r], 1)
                if r in sums:
                    dve.wait_ge(picked[r], G * UNITS + 1)
                    fold(BATCHES, 0, 1, X if r == 0 else D)
                else:
                    scan(G * UNITS, 0, 1, REST)

                if r == 0:
                    dve.wait_ge(counted, UNITS + 1)
                    dve.tensor_tensor_scan(base_f[:], iota_1[0:1, 0:1].to_broadcast([1, TILES]), ps[0:1, COUNT:COUNT + TILES], 0.0,
                                           ALU.mult, ALU.add).then_inc(count_steps, 1)
                    dve.wait_ge(count_steps, 1)
                    dve.tensor_tensor(base_f[:], base_f[:], ps[0:1, COUNT:COUNT + TILES], ALU.subtract).then_inc(count_steps, 1)
                    dve.wait_ge(count_steps, 2)
                    dve.tensor_copy(node_base[:], base_f[:]).then_inc(count_steps, 1)

                dve.wait_ge(folded[r], COLS)

                lag = LAG_SPREAD[r]
                if r in projected:
                    dve.memset(hT[D:D + 1], 1.0).then_inc(dve_go, 1)

                def spread_of(k, s):
                    dve.wait_ge(rel_ready[r], k + 1)
                    if after(k, 2):
                        dve.wait_ge(spread_ps[r], k - 1)
                    for j in range(POOL_HOTS[r], CHUNK):
                        dve.tensor_scalar(spread_c[:, s, j, :], iota_1[:, :], rel_c[:, s, j:j + 1],
                                          None, ALU.is_equal).then_inc(spread_1h_dve[r], 1)

                def nodes(k, s):
                    if r == 0 and has(k, 0):
                        dve.wait_ge(win_sb[0], k + 1)
                        if after(k, 2):
                            dve.wait_ge(spread_1h[0], (k - 1) * POOL_HOTS[0])
                            dve.wait_ge(spread_1h_dve[0], (k - 1) * (CHUNK - POOL_HOTS[0]))
                        at = bass.ds(k * CHUNK, CHUNK)
                        dve.tensor_tensor(rel_c[:, s], win_c[:, s, :, D + 1], tile_at[:, at],
                                          ALU.subtract).then_inc(rel_ready[0], 1)
                        dve.tensor_tensor(node_rel[:, at], win_c[:, s, :, D + 1], tile_at[:, at],
                                          ALU.subtract).then_inc(dve_go, 1)
                    if r in projected and has(k, LAG_PROD[r]):
                        q, qs = k - LAG_PROD[r], (s + LAG_PROD[r]) % 2
                        dve.wait_ge(ht_ps[r], q + 1)
                        if after(q, 2):
                            dve.wait_ge(prod[r], q - 1)
                        dve.tensor_copy(hT[0:D, qs, :], ps[0:D, TRANS:TRANS + CHUNK * P]).then_inc(ht_sb[r], 1)
                    if r == 1 and has(k, 1):
                        invert(1, k - 1, 1 - s)
                    if r in spread_1h_dve:
                        if lag == 0:
                            if known(k) and k == 0:
                                spread_of(0, 0)
                            if not known(k) or k + 1 < CHUNKS:
                                spread_of(k + 1, 1 - s)
                        elif has(k, 0):
                            spread_of(k, s)
                    if not has(k, lag):
                        return
                    q, qs = k - lag, (s + lag) % 2
                    n = STEPS[r]

                    def a(ins, done):
                        ins.then_inc(stepA[r], 1)
                        if done < n:
                            dve.wait_ge(stepA[r], q * n + done)

                    dve.wait_ge(spread_ps[r], q + 1)
                    sv = ps[:, SPREAD[r][qs]:SPREAD[r][qs] + CHUNK * P].rearrange("p (t c) -> p t c", c=P)
                    agg, here = sv[:, :, 0:D], chunk(xs, q)
                    at = bass.ds(q * CHUNK, CHUNK)
                    by = scale[:, at].unsqueeze(2).to_broadcast([P, CHUNK, D])
                    if after(q, 1):
                        dve.wait_ge(stepA[r], q * n)
                    if r == 0:
                        a(dve.tensor_scalar(scale[:, at], sv[:, :, D], 1.0, None, ALU.max), 1)
                        dve.sem_inc(dve_go, 1)
                        a(dve.reciprocal(scale[:, at], scale[:, at]), 2)
                        if after(q, 2):
                            dve.wait_ge(tstored[1][qs], (q - qs) * 8)
                        a(dve.tensor_tensor(nout[:, qs], agg, by, ALU.mult), 3)
                        a(dve.scalar_tensor_tensor(here, nout[:, qs], 0.5, here, ALU.mult, ALU.add), 4)
                    elif r == 1:
                        a(dve.tensor_tensor(tmp[:], agg, by, ALU.mult), 1)
                        a(dve.scalar_tensor_tensor(here, tmp[:], 0.5, here, ALU.mult, ALU.add), 2)
                        dve.wait_ge(stepA[1], q * n + n)
                        stats_of(1, q, qs)
                    else:
                        if not after(q, 1):
                            dve.wait_ge(root_sb[r - 1], CHUNKS)
                        a(dve.tensor_tensor(tmp[:], agg, chunk(root, q), ALU.add), 1)
                        if r == 2 and after(q, 2):
                            dve.wait_ge(ht_ps[2], q - 1)
                        a(dve.scalar_tensor_tensor(hbuf[:, qs], tmp[:], SLOPE, tmp[:], ALU.mult, ALU.max), 2)
                        if r == 3:
                            a(dve.tensor_tensor(here, here, hbuf[:, qs], ALU.add), 3)

                pipeline(dve, nodes, LAGS[r])


_INS = ["x", "srcs", "cur", "prev", "nxt", "eat", "W1_msg", "W1_edge", "W1_root", "b1",
        "W2_msg", "W2_edge", "W2_root", "b2"]


def kernel(x, src, dst, edge_attr_32, L1_gnn_W1_msg, L1_gnn_W1_edge, L1_gnn_W1_root, L1_gnn_b1,
           L1_gnn_W2_msg, L1_gnn_W2_edge, L1_gnn_W2_root, L1_gnn_b2):
    import concourse.bacc as bacc
    from concourse.bass_utils import run_bass_kernel_spmd as run

    def by_batch(v):
        return np.ascontiguousarray(v.reshape(COLS, P).T)

    fill = COLS * P - E
    srcs = by_batch(np.pad(np.asarray(src), (0, fill)))
    dsts = np.pad(np.pad(np.asarray(dst), (1, 0), constant_values=-1), (0, fill + 1), constant_values=-2)
    prev, cur, nxt = (by_batch(dsts[k:k + COLS * P]) for k in range(3))
    eat = np.ascontiguousarray(np.asarray(edge_attr_32).T)
    values = [x, srcs, cur, prev, nxt, eat, L1_gnn_W1_msg, L1_gnn_W1_edge, L1_gnn_W1_root, L1_gnn_b1,
              L1_gnn_W2_msg, L1_gnn_W2_edge, L1_gnn_W2_root, L1_gnn_b2]
    nc = bacc.Bacc("TRN2", target_bir_lowering=False, num_devices=1)
    arrays, args = {}, []
    for name, value in zip(_INS, values):
        a = np.ascontiguousarray(value)
        arrays[f"in_{name}"] = a
        args.append(nc.dram_tensor(f"in_{name}", a.shape, mybir.dt.from_np(a.dtype), kind="ExternalInput").ap())
    args.append(nc.dram_tensor("out_0", (N, D), F32, kind="ExternalOutput").ap())
    gnn(nc, *args)
    r = run(nc, [arrays], core_ids=[0])
    return r.results[0]["out_0"]
```
